# Optimizing a Trainium2 kernel written in Bass

```python
import numpy as np
import jax
import jax.numpy as jnp

def _softmax(x, axis=-1):
    return jax.nn.softmax(x, axis=axis)

def _gelu(x):
    return jax.nn.gelu(x, approximate=True)

def _silu(x):
    return jax.nn.silu(x)

def _sigmoid(x):
    return jax.nn.sigmoid(x)

def _layernorm(x, axis=-1, eps=1e-05):
    m = jnp.mean(x, axis=axis, keepdims=True)
    v = jnp.var(x, axis=axis, keepdims=True)
    return (x - m) / jnp.sqrt(v + eps)

def _scatter_add(tgt, idx, src, axis=0):
    return tgt.at[idx].add(src)

def _segment_sum(src, seg, n):
    return jax.ops.segment_sum(src, seg, n)
kernel_name = 'mk_gnn_resnorm_d4_gnn_r8_a5fcfe'

def setup_inputs(seed: int=0):
    np.random.seed(seed)
    _w = jnp.asarray

    def _rec_inputs():
        import jax
        import jax.numpy as jnp
        _gk = jax.random.key(seed)
        x = -0.000202 + 1 * jax.random.normal(jax.random.fold_in(_gk, 1), (6250, 128), jnp.float32)
        src = jax.random.randint(jax.random.fold_in(_gk, 2), (100000,), 0, 6250, jnp.int32)
        dst = jnp.minimum((6250 * jax.random.uniform(jax.random.fold_in(_gk, 3), (100000,)) ** 2.0).astype(jnp.int32), 49999)
        _o = jnp.argsort(dst, stable=True)
        src = src[_o]
        dst = dst[_o]
        edge_attr_16 = 0.000669165 + 0.999965 * jax.random.normal(jax.random.fold_in(_gk, 11), (100000, 16), jnp.float32)
        edge_attr_64 = 0.000189758 + 1.00013 * jax.random.normal(jax.random.fold_in(_gk, 12), (100000, 64), jnp.float32)
        edge_type_4 = jax.random.randint(jax.random.fold_in(_gk, 14), (100000,), 0, 4, jnp.int32)
        return (x, src, dst, edge_attr_16, edge_attr_64, edge_type_4)
    x, src, dst, edge_attr_16, edge_attr_64, edge_type_4 = _rec_inputs()

    def _L0_gnn_setup():
        import jax, jax.numpy as jnp
        import numpy as np
        N = 6250
        E = 100000
        IN_DIM = 128
        OUT_DIM = 128
        BN_EPS = 1e-05

        def _bn(h, gamma, beta):
            mean = jnp.mean(h, axis=0)
            var = jnp.mean(jnp.square(h - mean), axis=0)
            return (h - mean) * jax.lax.rsqrt(var + BN_EPS) * gamma + beta

        def _prelu(h, a):
            return jnp.where(h >= 0, h, a * h)
        key = jax.random.key(seed)
        ks = jax.random.split(key, 8)
        x = jax.random.normal(ks[0], (N, IN_DIM), dtype=jnp.float32)
        edge_index = jax.random.randint(ks[1], (2, E), 0, N, dtype=jnp.int64)
        s1 = 1.0 / np.sqrt(IN_DIM)
        s2 = 1.0 / np.sqrt(OUT_DIM)
        return {'x': x, 'edge_index': edge_index, 'eps': jnp.zeros((), dtype=jnp.float32), 'W1': jax.random.uniform(ks[2], (IN_DIM, OUT_DIM), jnp.float32, -s1, s1), 'b1': jax.random.uniform(ks[3], (OUT_DIM,), jnp.float32, -s1, s1), 'gamma1': jnp.ones((OUT_DIM,), jnp.float32), 'beta1': jnp.zeros((OUT_DIM,), jnp.float32), 'a1': jnp.full((), 0.25, jnp.float32), 'W2': jax.random.uniform(ks[4], (OUT_DIM, OUT_DIM), jnp.float32, -s2, s2), 'b2': jax.random.uniform(ks[5], (OUT_DIM,), jnp.float32, -s2, s2), 'gamma2': jnp.ones((OUT_DIM,), jnp.float32), 'beta2': jnp.zeros((OUT_DIM,), jnp.float32), 'a2': jnp.full((), 0.25, jnp.float32)}
    _L0_gnn_all = _L0_gnn_setup()
    _L0_gnn_in = {k: v for k, v in _L0_gnn_all.items() if k in ('eps', 'W1', 'b1', 'gamma1', 'beta1', 'a1', 'W2', 'b2', 'gamma2', 'beta2', 'a2')}
    del _L0_gnn_all

    def _L1_gnn_setup():
        import jax, jax.numpy as jnp
        import numpy as np
        N = 6250
        E = 100000
        D_IN = 128
        D_NODE = 128
        D_EIN = 64
        D_EDGE = 128
        L = 2
        NEG_SLOPE = 0.2

        def _gat_conv(h, src, dst, W, a_src, a_dst, bias):
            g = h @ W
            s = (g * a_src).sum(-1)
            d = (g * a_dst).sum(-1)
            e = jax.nn.leaky_relu(s[src] + d[dst], NEG_SLOPE)
            m = jax.ops.segment_max(e, dst, num_segments=N)
            m = jnp.where(jnp.isfinite(m), m, 0.0)
            ex = jnp.exp(e - m[dst])
            z = jax.ops.segment_sum(ex, dst, num_segments=N)
            alpha = ex / z[dst]
            out = jax.ops.segment_sum(g[src] * alpha[:, None], dst, num_segments=N)
            return out + bias
        key = jax.random.key(seed)
        ks = jax.random.split(key, 12)
        s = 0.05
        return {'x': jax.random.normal(ks[0], (N, D_IN), jnp.float32), 'edge_index': jax.random.randint(ks[1], (2, E), 0, N), 'edge_attr': jax.random.normal(ks[2], (E, D_EIN), jnp.float32), 'W_node': jax.random.normal(ks[3], (D_IN, D_NODE), jnp.float32) * s, 'b_node': jnp.zeros((D_NODE,), jnp.float32), 'W_edge': jax.random.normal(ks[4], (D_EIN, D_EDGE), jnp.float32) * s, 'b_edge': jnp.zeros((D_EDGE,), jnp.float32), 'lyr_We': jax.random.normal(ks[5], (L, D_EDGE, D_NODE), jnp.float32) * s, 'lyr_be': jnp.zeros((L, D_NODE), jnp.float32), 'lyr_W': jax.random.normal(ks[6], (L, D_NODE, D_NODE), jnp.float32) * s, 'att_src': jax.random.normal(ks[7], (L, D_NODE), jnp.float32) * s, 'att_dst': jax.random.normal(ks[8], (L, D_NODE), jnp.float32) * s, 'lyr_bias': jnp.zeros((L, D_NODE), jnp.float32)}
    _L1_gnn_all = _L1_gnn_setup()
    _L1_gnn_in = {k: v for k, v in _L1_gnn_all.items() if k in ('W_node', 'b_node', 'W_edge', 'b_edge', 'lyr_We', 'lyr_be', 'lyr_W', 'att_src', 'att_dst', 'lyr_bias')}
    del _L1_gnn_all

    def _L2_gnn_setup():
        import jax, jax.numpy as jnp
        import numpy as np
        EPS = 1e-05
        NEG_SLOPE = 0.2

        def _layernorm(x, g, b):
            mu = x.mean(-1, keepdims=True)
            var = ((x - mu) ** 2).mean(-1, keepdims=True)
            return (x - mu) * jax.lax.rsqrt(var + EPS) * g + b

        def _forward(h, edge_attr, rel_emb, W_l, b_l, W_r, b_r, W_e, att, bias, gate, g1, bt1, g2, bt2, Wf1, bf1, Wf2, bf2, edge_index, edge_type):
            N, F = h.shape
            R, H, C = att.shape
            HC = H * C
            E = edge_type.shape[0]
            De = edge_attr.shape[1]
            src, dst = (edge_index[0], edge_index[1])
            xl = jnp.einsum('nf,rfh->nrh', h, W_l) + b_l
            xr = jnp.einsum('nf,rfh->nrh', h, W_r) + b_r
            xl_e = xl[src, edge_type]
            xr_e = xr[dst, edge_type]
            e_feat = jnp.zeros((E, HC), dtype=h.dtype)
            for r in range(R):
                vr = edge_attr @ W_e[r, :De] + rel_emb[r] @ W_e[r, De:]
                e_feat = jnp.where((edge_type == r)[:, None], vr, e_feat)
            x = jax.nn.leaky_relu(xl_e + xr_e + e_feat, NEG_SLOPE).reshape(E, H, C)
            score = jnp.einsum('ehc,ehc->eh', x, att[edge_type])
            seg = dst * R + edge_type
            m = jax.lax.stop_gradient(jax.ops.segment_max(score, seg, num_segments=N * R))
            alpha = jnp.exp(score - m[seg])
            denom = jax.ops.segment_sum(alpha, seg, num_segments=N * R)
            alpha = alpha / denom[seg]
            msg = (xl_e.reshape(E, H, C) * alpha[..., None]).reshape(E, HC)
            agg = jax.ops.segment_sum(msg, seg, num_segments=N * R).reshape(N, R, H, C)
            h_rel = agg.mean(axis=2) + bias
            gw = jax.nn.softmax(gate)
            h_msg = jnp.einsum('r,nrc->nc', gw, h_rel)
            h1 = _layernorm(h + h_msg, g1, bt1)
            ffn = jax.nn.silu(h1 @ Wf1 + bf1) @ Wf2 + bf2
            return _layernorm(h1 + ffn, g2, bt2)
        key = jax.random.key(seed)
        ks = jax.random.split(key, 16)
        N, F, E, De, Dr, R, H = (5000, 128, 18750, 16, 8, 4, 4)
        C = F
        HC = H * C
        FFN = int(F * 2.0)
        s = 0.05
        return {'h': jax.random.normal(ks[0], (N, F), jnp.float32), 'edge_index': jax.random.randint(ks[1], (2, E), 0, N), 'edge_attr': jax.random.normal(ks[2], (E, De), jnp.float32), 'edge_type': jax.random.randint(ks[3], (E,), 0, R), 'rel_emb': jax.random.normal(ks[4], (R, Dr), jnp.float32) * s, 'W_l': jax.random.normal(ks[5], (R, F, HC), jnp.float32) * s, 'b_l': jnp.zeros((R, HC), jnp.float32), 'W_r': jax.random.normal(ks[6], (R, F, HC), jnp.float32) * s, 'b_r': jnp.zeros((R, HC), jnp.float32), 'W_e': jax.random.normal(ks[7], (R, De + Dr, HC), jnp.float32) * s, 'att': jax.random.normal(ks[8], (R, H, C), jnp.float32) * s, 'bias': jnp.zeros((R, C), jnp.float32), 'gate': jax.random.normal(ks[9], (R,), jnp.float32) * 0.5, 'g1': jnp.ones((F,), jnp.float32), 'bt1': jnp.zeros((F,), jnp.float32), 'g2': jnp.ones((F,), jnp.float32), 'bt2': jnp.zeros((F,), jnp.float32), 'Wf1': jax.random.normal(ks[10], (F, FFN), jnp.float32) * s, 'bf1': jnp.zeros((FFN,), jnp.float32), 'Wf2': jax.random.normal(ks[11], (FFN, F), jnp.float32) * s, 'bf2': jnp.zeros((F,), jnp.float32)}
    _L2_gnn_all = _L2_gnn_setup()
    _L2_gnn_in = {k: v for k, v in _L2_gnn_all.items() if k in ('rel_emb', 'W_l', 'b_l', 'W_r', 'b_r', 'W_e', 'att', 'bias', 'gate', 'g1', 'bt1', 'g2', 'bt2', 'Wf1', 'bf1', 'Wf2', 'bf2')}
    del _L2_gnn_all

    def _L3_gnn_setup():
        import jax, jax.numpy as jnp
        import numpy as np
        N_NODES = 12500
        key = jax.random.key(seed)
        k1, k2, k3 = jax.random.split(key, 3)
        x = jax.random.normal(k1, (N_NODES, 128), dtype=jnp.float32)
        edge_index = jax.random.randint(k2, (2, 200000), 0, N_NODES, dtype=jnp.int64)
        W = jax.random.normal(k3, (128, 128), dtype=jnp.float32) * (1.0 / np.sqrt(128.0))
        b = jnp.zeros((128,), dtype=jnp.float32)
        return {'x': x, 'edge_index': edge_index, 'W': W, 'b': b}
    _L3_gnn_all = _L3_gnn_setup()
    _L3_gnn_in = {k: v for k, v in _L3_gnn_all.items() if k in ('W', 'b')}
    del _L3_gnn_all
    return {'x': x, 'src': src, 'dst': dst, 'edge_attr_16': edge_attr_16, 'edge_attr_64': edge_attr_64, 'edge_type_4': edge_type_4, 'L0_gnn_eps': _L0_gnn_in['eps'], 'L0_gnn_W1': _L0_gnn_in['W1'], 'L0_gnn_b1': _L0_gnn_in['b1'], 'L0_gnn_gamma1': _L0_gnn_in['gamma1'], 'L0_gnn_beta1': _L0_gnn_in['beta1'], 'L0_gnn_a1': _L0_gnn_in['a1'], 'L0_gnn_W2': _L0_gnn_in['W2'], 'L0_gnn_b2': _L0_gnn_in['b2'], 'L0_gnn_gamma2': _L0_gnn_in['gamma2'], 'L0_gnn_beta2': _L0_gnn_in['beta2'], 'L0_gnn_a2': _L0_gnn_in['a2'], 'L1_gnn_W_node': _L1_gnn_in['W_node'], 'L1_gnn_b_node': _L1_gnn_in['b_node'], 'L1_gnn_W_edge': _L1_gnn_in['W_edge'], 'L1_gnn_b_edge': _L1_gnn_in['b_edge'], 'L1_gnn_lyr_We': _L1_gnn_in['lyr_We'], 'L1_gnn_lyr_be': _L1_gnn_in['lyr_be'], 'L1_gnn_lyr_W': _L1_gnn_in['lyr_W'], 'L1_gnn_att_src': _L1_gnn_in['att_src'], 'L1_gnn_att_dst': _L1_gnn_in['att_dst'], 'L1_gnn_lyr_bias': _L1_gnn_in['lyr_bias'], 'L2_gnn_rel_emb': _L2_gnn_in['rel_emb'], 'L2_gnn_W_l': _L2_gnn_in['W_l'], 'L2_gnn_b_l': _L2_gnn_in['b_l'], 'L2_gnn_W_r': _L2_gnn_in['W_r'], 'L2_gnn_b_r': _L2_gnn_in['b_r'], 'L2_gnn_W_e': _L2_gnn_in['W_e'], 'L2_gnn_att': _L2_gnn_in['att'], 'L2_gnn_bias': _L2_gnn_in['bias'], 'L2_gnn_gate': _L2_gnn_in['gate'], 'L2_gnn_g1': _L2_gnn_in['g1'], 'L2_gnn_bt1': _L2_gnn_in['bt1'], 'L2_gnn_g2': _L2_gnn_in['g2'], 'L2_gnn_bt2': _L2_gnn_in['bt2'], 'L2_gnn_Wf1': _L2_gnn_in['Wf1'], 'L2_gnn_bf1': _L2_gnn_in['bf1'], 'L2_gnn_Wf2': _L2_gnn_in['Wf2'], 'L2_gnn_bf2': _L2_gnn_in['bf2'], 'L3_gnn_W': _L3_gnn_in['W'], 'L3_gnn_b': _L3_gnn_in['b']}

def reference(x, src, dst, edge_attr_16, edge_attr_64, edge_type_4, L0_gnn_eps, L0_gnn_W1, L0_gnn_b1, L0_gnn_gamma1, L0_gnn_beta1, L0_gnn_a1, L0_gnn_W2, L0_gnn_b2, L0_gnn_gamma2, L0_gnn_beta2, L0_gnn_a2, L1_gnn_W_node, L1_gnn_b_node, L1_gnn_W_edge, L1_gnn_b_edge, L1_gnn_lyr_We, L1_gnn_lyr_be, L1_gnn_lyr_W, L1_gnn_att_src, L1_gnn_att_dst, L1_gnn_lyr_bias, L2_gnn_rel_emb, L2_gnn_W_l, L2_gnn_b_l, L2_gnn_W_r, L2_gnn_b_r, L2_gnn_W_e, L2_gnn_att, L2_gnn_bias, L2_gnn_gate, L2_gnn_g1, L2_gnn_bt1, L2_gnn_g2, L2_gnn_bt2, L2_gnn_Wf1, L2_gnn_bf1, L2_gnn_Wf2, L2_gnn_bf2, L3_gnn_W, L3_gnn_b):
    import jax
    import jax.numpy as jnp

    def _L0_gnn_ref(x, edge_index, eps, W1, b1, gamma1, beta1, a1, W2, b2, gamma2, beta2, a2):
        import jax, jax.numpy as jnp
        import numpy as np
        N = 6250
        E = 100000
        IN_DIM = 128
        OUT_DIM = 128
        BN_EPS = 1e-05

        def _bn(h, gamma, beta):
            mean = jnp.mean(h, axis=0)
            var = jnp.mean(jnp.square(h - mean), axis=0)
            return (h - mean) * jax.lax.rsqrt(var + BN_EPS) * gamma + beta

        def _prelu(h, a):
            return jnp.where(h >= 0, h, a * h)
        src, dst = (edge_index[0], edge_index[1])
        agg = jax.ops.segment_sum(x[src], dst, num_segments=N)
        h = (1.0 + eps) * x + agg
        h = _prelu(_bn(h @ W1 + b1, gamma1, beta1), a1)
        h = _prelu(_bn(h @ W2 + b2, gamma2, beta2), a2)
        return h

    def _L1_gnn_ref(x, edge_index, edge_attr, W_node, b_node, W_edge, b_edge, lyr_We, lyr_be, lyr_W, att_src, att_dst, lyr_bias):
        import jax, jax.numpy as jnp
        import numpy as np
        N = 6250
        E = 100000
        D_IN = 128
        D_NODE = 128
        D_EIN = 64
        D_EDGE = 128
        L = 2
        NEG_SLOPE = 0.2

        def _gat_conv(h, src, dst, W, a_src, a_dst, bias):
            g = h @ W
            s = (g * a_src).sum(-1)
            d = (g * a_dst).sum(-1)
            e = jax.nn.leaky_relu(s[src] + d[dst], NEG_SLOPE)
            m = jax.ops.segment_max(e, dst, num_segments=N)
            m = jnp.where(jnp.isfinite(m), m, 0.0)
            ex = jnp.exp(e - m[dst])
            z = jax.ops.segment_sum(ex, dst, num_segments=N)
            alpha = ex / z[dst]
            out = jax.ops.segment_sum(g[src] * alpha[:, None], dst, num_segments=N)
            return out + bias
        h = x @ W_node + b_node
        ea = edge_attr @ W_edge + b_edge
        src, dst = (edge_index[0], edge_index[1])
        loop = jnp.arange(N)
        src_sl = jnp.concatenate([src, loop])
        dst_sl = jnp.concatenate([dst, loop])
        for l in range(L):
            _ = ea @ lyr_We[l] + lyr_be[l]
            h = _gat_conv(h, src_sl, dst_sl, lyr_W[l], att_src[l], att_dst[l], lyr_bias[l])
        return h

    def _L2_gnn_ref(h, edge_index, edge_attr, edge_type, rel_emb, W_l, b_l, W_r, b_r, W_e, att, bias, gate, g1, bt1, g2, bt2, Wf1, bf1, Wf2, bf2):
        import jax, jax.numpy as jnp
        import numpy as np
        EPS = 1e-05
        NEG_SLOPE = 0.2

        def _layernorm(x, g, b):
            mu = x.mean(-1, keepdims=True)
            var = ((x - mu) ** 2).mean(-1, keepdims=True)
            return (x - mu) * jax.lax.rsqrt(var + EPS) * g + b

        def _forward(h, edge_attr, rel_emb, W_l, b_l, W_r, b_r, W_e, att, bias, gate, g1, bt1, g2, bt2, Wf1, bf1, Wf2, bf2, edge_index, edge_type):
            N, F = h.shape
            R, H, C = att.shape
            HC = H * C
            E = edge_type.shape[0]
            De = edge_attr.shape[1]
            src, dst = (edge_index[0], edge_index[1])
            xl = jnp.einsum('nf,rfh->nrh', h, W_l) + b_l
            xr = jnp.einsum('nf,rfh->nrh', h, W_r) + b_r
            xl_e = xl[src, edge_type]
            xr_e = xr[dst, edge_type]
            e_feat = jnp.zeros((E, HC), dtype=h.dtype)
            for r in range(R):
                vr = edge_attr @ W_e[r, :De] + rel_emb[r] @ W_e[r, De:]
                e_feat = jnp.where((edge_type == r)[:, None], vr, e_feat)
            x = jax.nn.leaky_relu(xl_e + xr_e + e_feat, NEG_SLOPE).reshape(E, H, C)
            score = jnp.einsum('ehc,ehc->eh', x, att[edge_type])
            seg = dst * R + edge_type
            m = jax.lax.stop_gradient(jax.ops.segment_max(score, seg, num_segments=N * R))
            alpha = jnp.exp(score - m[seg])
            denom = jax.ops.segment_sum(alpha, seg, num_segments=N * R)
            alpha = alpha / denom[seg]
            msg = (xl_e.reshape(E, H, C) * alpha[..., None]).reshape(E, HC)
            agg = jax.ops.segment_sum(msg, seg, num_segments=N * R).reshape(N, R, H, C)
            h_rel = agg.mean(axis=2) + bias
            gw = jax.nn.softmax(gate)
            h_msg = jnp.einsum('r,nrc->nc', gw, h_rel)
            h1 = _layernorm(h + h_msg, g1, bt1)
            ffn = jax.nn.silu(h1 @ Wf1 + bf1) @ Wf2 + bf2
            return _layernorm(h1 + ffn, g2, bt2)
        return _forward(h, edge_attr, rel_emb, W_l, b_l, W_r, b_r, W_e, att, bias, gate, g1, bt1, g2, bt2, Wf1, bf1, Wf2, bf2, edge_index, edge_type)

    def _L3_gnn_ref(x, edge_index, W, b):
        import jax, jax.numpy as jnp
        import numpy as np
        N_NODES = 12500
        N = x.shape[0]
        loop = jnp.arange(N, dtype=edge_index.dtype)
        src = jnp.concatenate([edge_index[0], loop])
        dst = jnp.concatenate([edge_index[1], loop])
        ones = jnp.ones(src.shape[0], dtype=x.dtype)
        deg = jax.ops.segment_sum(ones, dst, num_segments=N)
        deg_inv_sqrt = jnp.where(deg > 0, jax.lax.rsqrt(jnp.maximum(deg, 1.0)), 0.0)
        norm = deg_inv_sqrt[src] * deg_inv_sqrt[dst]
        h = x @ W
        msg = h[src] * norm[:, None]
        out = jax.ops.segment_sum(msg, dst, num_segments=N) + b
        return jax.nn.relu(out)
    edge_index = jnp.stack([src, dst])
    x = _layernorm(x + _L0_gnn_ref(x, edge_index, L0_gnn_eps, L0_gnn_W1, L0_gnn_b1, L0_gnn_gamma1, L0_gnn_beta1, L0_gnn_a1, L0_gnn_W2, L0_gnn_b2, L0_gnn_gamma2, L0_gnn_beta2, L0_gnn_a2), axis=-1)
    x = _layernorm(x + _L1_gnn_ref(x, edge_index, edge_attr_64, L1_gnn_W_node, L1_gnn_b_node, L1_gnn_W_edge, L1_gnn_b_edge, L1_gnn_lyr_We, L1_gnn_lyr_be, L1_gnn_lyr_W, L1_gnn_att_src, L1_gnn_att_dst, L1_gnn_lyr_bias), axis=-1)
    x = _layernorm(x + _L2_gnn_ref(x, edge_index, edge_attr_16, edge_type_4, L2_gnn_rel_emb, L2_gnn_W_l, L2_gnn_b_l, L2_gnn_W_r, L2_gnn_b_r, L2_gnn_W_e, L2_gnn_att, L2_gnn_bias, L2_gnn_gate, L2_gnn_g1, L2_gnn_bt1, L2_gnn_g2, L2_gnn_bt2, L2_gnn_Wf1, L2_gnn_bf1, L2_gnn_Wf2, L2_gnn_bf2), axis=-1)
    x = _layernorm(x + _L3_gnn_ref(x, edge_index, L3_gnn_W, L3_gnn_b), axis=-1)
    return x

_drawn_inputs = setup_inputs


def setup_inputs(seed=0):
    import zlib

    import numpy as np

    out = dict(_drawn_inputs(seed))
    spreads = {'L0_gnn_gamma1': (1.0, 0.2),
     'L0_gnn_beta1': (0.0, 0.1),
     'L0_gnn_gamma2': (1.0, 0.2),
     'L0_gnn_beta2': (0.0, 0.1),
     'L1_gnn_b_node': (0.0, 0.1),
     'L1_gnn_b_edge': (0.0, 0.1),
     'L1_gnn_lyr_be': (0.0, 0.1),
     'L1_gnn_lyr_bias': (0.0, 0.1),
     'L2_gnn_b_l': (0.0, 0.452),
     'L2_gnn_b_r': (0.0, 2.0),
     'L2_gnn_bias': (0.0, 0.1),
     'L2_gnn_g1': (1.0, 0.2),
     'L2_gnn_bt1': (0.0, 0.1),
     'L2_gnn_g2': (1.0, 0.2),
     'L2_gnn_bt2': (0.0, 0.1),
     'L2_gnn_bf1': (0.0, 0.391),
     'L2_gnn_bf2': (0.0, 0.1),
     'L3_gnn_b': (0.0, 0.1)}
    factors = {'edge_attr_16': 8.0,
     'L0_gnn_b1': 64.0,
     'L0_gnn_b2': 64.0,
     'L1_gnn_att_src': 8.0,
     'L1_gnn_att_dst': 64.0,
     'L2_gnn_rel_emb': 64.0,
     'L2_gnn_W_r': 8.0,
     'L2_gnn_W_e': 8.0,
     'L2_gnn_att': 8.0,
     'L2_gnn_gate': 3.784}
    for name, (base, spread) in spreads.items():
        noise = np.random.default_rng([zlib.crc32(name.encode()), seed]).standard_normal(out[name].shape)
        drawn = base * np.exp(spread * noise) if base else spread * noise
        out[name] = jnp.asarray(drawn.astype(out[name].dtype))
    for name, factor in factors.items():
        out[name] = (out[name] * factor).astype(out[name].dtype)
    return out
```

```python
from contextlib import ExitStack

import numpy as np

import concourse.bass as bass
import concourse.mybir as mybir

F32 = mybir.dt.float32
I32 = mybir.dt.int32
ALU = mybir.AluOpType
ACT = mybir.ActivationFunctionType
AX_X = mybir.AxisListType.X
ENG = mybir.EngineType

P = 128
N, E, F = 6250, 100000, 128
NB = -(-N // P)
NP = NB * P
LAST = N - (NB - 1) * P
BATCH = 8
TILES = -(-((E + NB * (P - 1)) // P) // BATCH) * BATCH
G = -(-TILES // P)
SLOTS = G * P
IT = P * G
EP = -(-(E + P) // P) * P
EC = EP // P
CH = 448
R, H, HC, DE, DR = 4, 4, 512, 16, 8
ROW = 130
BIG = 1e38
FAR = 1 << 20
LN_EPS = 1e-5

REG_WHY = "made on chip from counts whose range the shapes fix"


class Sem:

    def __init__(self, handle):
        self.handle, self.count = handle, 0


class Stage:

    ENGINES = ("sync", "scalar", "gpsimd", "tensor", "vector")

    def __init__(self, nc, ctx, name):
        self.nc, self.ctx, self.name = nc, ctx, name
        self.queue = {e: [] for e in self.ENGINES}
        self.done = {}

    def do(self, engine, emit, after=()):
        if engine not in self.done:
            self.done[engine] = Sem(self.ctx.enter_context(self.nc.semaphore(f"{self.name}_{engine}")))
        sem = self.done[engine]
        sem.count += 1
        self.queue[engine].append((emit, list(flat(after)), sem, 1))
        return (sem, sem.count)

    def v(self, emit, *after):
        return self.do("vector", emit, after)

    def s(self, emit, *after):
        return self.do("scalar", emit, after)

    def t(self, emit, *after):
        return self.do("tensor", emit, after)

    def g(self, emit, *after):
        return self.do("gpsimd", emit, after)

    def dma(self, engine, emit, sem, *after):
        sem.count += 16
        self.queue[engine].append((emit, list(flat(after)), sem, 16))
        return (sem, sem.count)

    def plain(self, engine, emit, *after):
        self.queue[engine].append((emit, list(flat(after)), None, 0))

    def wait(self, engine, *after):
        self.queue[engine].append((None, list(flat(after)), None, 0))

    def run(self):
        def play(name):
            def body(eng):
                seen = {}
                for emit, after, sem, inc in self.queue[name]:
                    for ticket in after:
                        if seen.get(ticket[0], 0) < ticket[1]:
                            eng.wait_ge(ticket[0].handle, ticket[1])
                            seen[ticket[0]] = ticket[1]
                    if emit is not None:
                        made = emit(eng)
                        if sem is not None:
                            made.then_inc(sem.handle, inc)
            return body

        with self.nc.Block() as block:
            for name in self.ENGINES:
                if self.queue[name]:
                    getter = {"sync": block.sync, "scalar": block.scalar, "gpsimd": block.gpsimd,
                              "tensor": block.tensor, "vector": block.vector}[name]
                    getter(play(name))


def flat(tickets):
    for x in tickets:
        if x is None:
            continue
        if isinstance(x, tuple) and len(x) == 2 and isinstance(x[0], Sem):
            yield x
        else:
            yield from flat(x)


class Ring:

    def __init__(self, items):
        self.items, self.free, self.n = items, [None] * len(items), -1

    def take(self):
        self.n += 1
        k = self.n % len(self.items)
        return k, self.items[k], self.free[k]


class Kernel:
    def __init__(self, nc, ctx):
        self.nc, self.ctx, self.named = nc, ctx, {}
        self.psum = [ctx.enter_context(nc.psum_tensor(f"bank{k}", [P, 512], F32)) for k in range(8)]
        self.dma_sems = [Sem(ctx.enter_context(nc.semaphore(f"dma{k}"))) for k in range(16)]
        self.pool_sems = [Sem(ctx.enter_context(nc.semaphore(f"pool_dma{k}"))) for k in range(8)]

    def stage(self, name):
        return Stage(self.nc, self.ctx, name)

    def sb(self, name, cols, dt=F32, rows=P, ctx=None):
        self.named[name] = self.named.get(name, 0) + 1
        if self.named[name] > 1:
            name = f"{name}_{self.named[name]}"
        return (ctx or self.ctx).enter_context(self.nc.sbuf_tensor(name, [rows, cols], dt))

    def regs(self, engine, row, first, count, top):
        return self.nc.values_load_multi_w_load_instructions(
            row[0:1, first:first + count], engines=[engine], min_val=0, max_val=top,
            skip_runtime_bounds_check_because=REG_WHY)[1]


def blocks3(t, w=F):
    return t[:, :].rearrange("p (b f) -> p b f", f=w)


def over(col, w):
    return col.unsqueeze(2).to_broadcast([col.shape[0], col.shape[1], w])


def make_constants(k):
    c = {}
    for name in ("ident", "before", "shift_up", "shift_down", "ones"):
        c[name] = k.sb(name, P)
    c["node_iota"] = k.sb("node_iota", P)
    c["slot_col"] = k.sb("slot_col", 1)
    st = k.stage("constants")
    tmp = k.sb("iota_int", P + 1, I32)
    zero = [st.g(lambda e, t=c[n]: e.memset(t[:, :], 0.0)) for n in ("ident", "shift_up", "shift_down")]
    one = [st.g(lambda e, t=c[n]: e.memset(t[:, :], 1.0)) for n in ("ones", "before")]

    def select(t, op, base, step, chan, fill, after):
        return st.g(lambda e: e.affine_select(out=t[:, :], in_=t[:, :], pattern=[[step, P]], compare_op=op,
                                              fill=fill, base=base, channel_multiplier=chan), after)
    select(c["ident"], ALU.not_equal, 0, 1, -1, 1.0, zero)
    select(c["shift_up"], ALU.not_equal, -1, 1, -1, 1.0, zero)
    select(c["shift_down"], ALU.not_equal, 1, 1, -1, 1.0, zero)
    select(c["before"], ALU.is_gt, 0, 1, -1, 0.0, one)
    a = st.g(lambda e: e.iota(tmp[:, 0:P], pattern=[[1, P]], base=0, channel_multiplier=0))
    b = st.g(lambda e: e.iota(tmp[:, P:P + 1], pattern=[[0, 1]], base=0, channel_multiplier=1))
    st.v(lambda e: e.tensor_copy(c["node_iota"][:, :], tmp[:, 0:P]), a)
    st.v(lambda e: e.tensor_copy(c["slot_col"][:, :], tmp[:, P:P + 1]), b)
    st.run()
    return c


def to_slots(k, st, c, out, src, after, banks=(0, 1)):
    view = out[:, :].rearrange("q (p g) -> q g p", g=G)
    done = []
    for bank, lo, hi in ((banks[0], 0, 4), (banks[1], 4, G)):
        ps = k.psum[bank]
        for g in range(lo, hi):
            t = st.t(lambda e, g=g, lo=lo, ps=ps: e.transpose(ps[:, (g - lo) * P:(g - lo + 1) * P], src(g),
                                                              c["ident"][:, :]), after)
        done.append(st.v(lambda e, lo=lo, hi=hi, ps=ps: e.tensor_copy(
            view[:, lo:hi, :], ps[:, 0:(hi - lo) * P].rearrange("q (g p) -> q g p", p=P)), t))
    return done


def to_scan(k, st, c, out, src, after, banks=(0, 1)):
    view = src.rearrange("q (p g) -> q g p", g=G)
    done = []
    for bank, lo, hi in ((banks[0], 0, 4), (banks[1], 4, G)):
        ps = k.psum[bank]
        for g in range(lo, hi):
            t = st.t(lambda e, g=g, lo=lo, ps=ps: e.transpose(ps[:, (g - lo) * P:(g - lo + 1) * P], view[:, g, :],
                                                              c["ident"][:, :]), after)
        done.append(st.v(lambda e, lo=lo, hi=hi, ps=ps: e.tensor_copy(
            out[:, lo * P:hi * P], ps[:, 0:(hi - lo) * P]), t))
    return done


def plan_tiles(k, c, dst_all, recs, ed):
    for n in ("acc_row", "blk_row", "edge_row"):
        ed[n] = k.sb(n, IT, I32, rows=1)
    ed["src"] = k.sb("src_idx", IT, I32)
    for n in ("local", "valid", "type", "dst"):
        ed[n] = k.sb("e_" + n, IT)
    for n in ("same_prev", "same_next", "type_scan", "add_prev", "add_next", "pre_mul", "suf_mul", "pre_add",
              "suf_add"):
        ed[n] = k.sb(n, SLOTS)
    ed["last"] = k.sb("last_slot", IT)
    ed["flags"] = k.sb("flag_rows", 4 * P, rows=R)
    with ExitStack() as own:
        sb = lambda n, w, dt=F32, rows=P: k.sb(n, w, dt, rows, own)
        st = k.stage("count")
        dst_i, dst_f, junk = sb("dst_i", EC, I32), sb("dst_f", EC), sb("junk", EC)
        cnt = sb("cnt", NB + 1)
        got = st.dma("sync", lambda e: e.dma_start(dst_i[:, :], dst_all.rearrange("(p j) -> p j", j=EC)), k.dma_sems[0])
        cast = st.v(lambda e: e.tensor_copy(dst_f[:, :], dst_i[:, :]), got)
        t = st.v(lambda e: e.memset(cnt[:, 0:1], 0.0))
        for b in range(1, NB + 1):
            t = st.v(lambda e, b=b: e.tensor_scalar(junk[:, :], dst_f[:, :], float(P * b), 0.0, ALU.is_lt, ALU.add,
                                                    accum_out=cnt[:, b:b + 1]), cast, t)
        ps = k.psum[0]
        st.t(lambda e: e.matmul(ps[0:NB, 0:1], cnt[:, 0:NB], c["ones"][:, 0:1], start=True, stop=True), t)
        m = st.t(lambda e: e.matmul(ps[0:NB, 1:2], cnt[:, 1:NB + 1], c["ones"][:, 0:1], start=True, stop=True))
        col = sb("block_cols", 8)
        coli = sb("block_cols_int", 2, I32)
        B = slice(0, NB)
        v = st.v(lambda e: e.tensor_copy(col[B, 0:2], ps[B, 0:2]), m)
        v = n_edges = st.v(lambda e: e.tensor_tensor(col[B, 2:3], col[B, 1:2], col[B, 0:1], ALU.subtract), v)
        v = st.v(lambda e: e.tensor_scalar(coli[B, 0:1], col[B, 2:3], float(P - 1), None, ALU.add), v)
        v = st.v(lambda e: e.tensor_scalar(coli[B, 1:2], coli[B, 0:1], 7, None, ALU.arith_shift_right), v)
        v = tiles = st.v(lambda e: e.tensor_copy(col[B, 3:4], coli[B, 1:2]), v)
        v = st.v(lambda e: e.scalar_tensor_tensor(out=col[B, 4:5], in0=col[B, 3:4], scalar=-float(P), in1=col[B, 2:3],
                                                  op0=ALU.mult, op1=ALU.add), v)
        st.t(lambda e: e.matmul(ps[0:NB, 2:3], c["before"][B, B], col[B, 3:4], start=True, stop=True), v)
        m = st.t(lambda e: e.matmul(ps[0:NB, 3:4], c["shift_up"][B, B], col[B, 4:5], start=True, stop=True))
        v = st.v(lambda e: e.tensor_copy(col[B, 5:7], ps[B, 2:4]), m)
        tile_i, tile_f = sb("tile_i", IT, I32), sb("tile_f", IT)
        ti = st.g(lambda e: e.iota(tile_i[:, :], pattern=[[1, IT]], base=0, channel_multiplier=0))
        tf = st.v(lambda e: e.tensor_copy(tile_f[:, :], tile_i[:, :]), ti)
        passed = sb("passed", IT)
        pas = st.v(lambda e: e.tensor_scalar(passed[B, :], tile_f[B, :], col[B, 5:6], None, ALU.is_ge), v, tf)
        w_jump, w_n = sb("w_jump", P), sb("w_n", P)
        w1 = st.v(lambda e: e.tensor_scalar(w_jump[B, :], c["ones"][B, :], col[B, 6:7], None, ALU.mult), v)
        w2 = st.v(lambda e: e.tensor_scalar(w_n[B, :], c["ones"][B, :], col[B, 2:3], None, ALU.mult), n_edges)
        half = IT // 2
        for j, w in enumerate((c["ones"], w_jump, w_n)):
            for h in range(2):
                m = st.t(lambda e, j=j, h=h, w=w: e.matmul(k.psum[1 + 2 * j + h][:, 0:half], w[B, :],
                                                           passed[B, h * half:(h + 1) * half], start=True, stop=True),
                         pas, w1, w2)
        blk, first, left, tmp = sb("t_blk", IT), sb("t_first", IT), sb("t_left", IT), sb("t_tmp", IT)
        outs = []
        for h in range(2):
            s = slice(h * half, (h + 1) * half)
            a = st.v(lambda e, s=s, h=h: e.tensor_scalar(blk[:, s], k.psum[1 + h][:, 0:half], -1.0, None, ALU.add), m)
            b_ = st.v(lambda e, s=s, h=h: e.scalar_tensor_tensor(
                out=first[:, s], in0=tile_f[:, s], scalar=float(P), in1=k.psum[3 + h][:, 0:half], op0=ALU.mult,
                op1=ALU.add), m, tf)
            b_ = st.v(lambda e, s=s: e.tensor_scalar(first[:, s], first[:, s], float(E), None, ALU.min), b_)
            b_ = st.v(lambda e, s=s, h=h: e.tensor_tensor(left[:, s], k.psum[5 + h][:, 0:half], first[:, s],
                                                          ALU.subtract), b_)
            outs += [a, b_]
        va = st.v(lambda e: e.tensor_scalar(ed["valid"][:, :], left[:, :], c["slot_col"][:, 0:1], None, ALU.is_gt), outs)
        st.v(lambda e: e.tensor_scalar(ed["acc_row"][:, :], blk[0:1, :], float(ROW), None, ALU.mult), outs)
        st.v(lambda e: e.tensor_scalar(ed["blk_row"][:, :], blk[0:1, :], float(P), None, ALU.mult), outs)
        st.v(lambda e: e.tensor_copy(ed["edge_row"][:, :], first[0:1, :]), outs)
        st.run()

        st = k.stage("records")
        rec_i, rec_f = sb("rec_i", G * P * 3, I32), sb("rec_f", G * P * 3)
        got = []
        for j in range(0, IT, BATCH):
            eng = ("sync", "scalar")[(j // BATCH) % 2]
            kind = (ENG.SP, ENG.Activation)[(j // BATCH) % 2]
            hold = []
            st.plain(eng, lambda e, j=j, kind=kind, hold=hold: hold.extend(k.regs(kind, ed["edge_row"], j, BATCH, E)))
            for n in range(BATCH):
                p, g = divmod(j + n, G)
                got = st.dma(eng, lambda e, p=p, g=g, n=n, hold=hold: e.dma_start(
                    rec_i[p:p + 1, g * 3 * P:(g + 1) * 3 * P], recs[:, :].rearrange("e c -> (e c)").unsqueeze(0)[
                        :, bass.ds(hold[n] * 3, 3 * P)]), k.dma_sems[1 + (j // BATCH) % 2])
                if eng == "sync":
                    got_sp = got
                else:
                    got_act = got
        cast = st.v(lambda e: e.tensor_copy(rec_f[:, :], rec_i[:, :]), got_sp, got_act)
        recv = rec_f[:, :].rearrange("p (g q c) -> p g q c", g=G, c=3)
        st.v(lambda e: e.tensor_copy(ed["type_scan"][:, :].rearrange("p (g q) -> p g q", g=G), recv[:, :, :, 2]), cast)
        srcf, key = sb("src_f", IT), sb("key", IT)
        a = to_slots(k, st, c, srcf, lambda g: recv[:, g, :, 0], [cast], (0, 1))
        b_ = to_slots(k, st, c, ed["dst"], lambda g: recv[:, g, :, 1], [cast], (2, 3))
        t_ = to_slots(k, st, c, ed["type"], lambda g: recv[:, g, :, 2], [cast], (4, 5))
        st.v(lambda e: e.tensor_tensor(ed["src"][:, :], srcf[:, :], ed["valid"][:, :], ALU.mult), a)
        x = st.v(lambda e: e.scalar_tensor_tensor(out=ed["dst"][:, :], in0=ed["dst"][:, :], scalar=1.0,
                                                  in1=ed["valid"][:, :], op0=ALU.add, op1=ALU.mult), b_)
        y = st.v(lambda e: e.tensor_tensor(tmp[:, :], blk[:, :], ed["valid"][:, :], ALU.mult))
        ky = st.v(lambda e: e.tensor_scalar(key[:, :], ed["dst"][:, :], -1.0, None, ALU.add), x)
        y = st.v(lambda e: e.scalar_tensor_tensor(out=ed["local"][:, :], in0=tmp[:, :], scalar=-float(P),
                                                  in1=key[:, :], op0=ALU.mult, op1=ALU.add), y, ky)
        st.v(lambda e: e.tensor_scalar(ed["dst"][:, :], key[:, :], 0.0, None, ALU.max), ky)
        kx = sb("key_scan", SLOTS + 2)
        kk = to_scan(k, st, c, kx[:, 1:SLOTS + 1], key[:, :], [ky], (6, 7))
        st.t(lambda e: e.matmul(k.psum[0][:, 0:1], c["shift_up"][:, :], kx[:, SLOTS:SLOTS + 1], start=True, stop=True), kk, a)
        m = st.t(lambda e: e.matmul(k.psum[0][:, 1:2], c["shift_down"][:, :], kx[:, 1:2], start=True, stop=True))
        st.v(lambda e: e.tensor_copy(kx[:, 0:1], k.psum[0][:, 0:1]), m)
        v = st.v(lambda e: e.tensor_copy(kx[:, SLOTS + 1:SLOTS + 2], k.psum[0][:, 1:2]), m)
        for same, add, mul, full, lo, back in (("same_prev", "add_prev", "pre_mul", "pre_add", 0, False),
                                               ("same_next", "add_next", "suf_mul", "suf_add", 2, True)):
            d = slice(None, None, -1) if back else slice(None)
            q = st.v(lambda e, same=same, lo=lo: e.tensor_tensor(ed[same][:, :], kx[:, 1:SLOTS + 1],
                                                                 kx[:, lo:lo + SLOTS], ALU.is_equal), v, kk)
            st.v(lambda e, same=same, add=add: e.tensor_scalar(ed[add][:, :], ed[same][:, :], -1.0, BIG, ALU.add,
                                                               ALU.mult), q)
            q = st.v(lambda e, same=same, mul=mul, d=d: e.tensor_tensor_scan(
                ed[mul][:, d], ed[same][:, d], ed[same][:, d], 1.0, ALU.mult, ALU.min), q)
            st.v(lambda e, mul=mul, full=full: e.tensor_scalar(ed[full][:, :], ed[mul][:, :], -1.0, BIG, ALU.add,
                                                               ALU.mult), q)
            if back:
                lst = sb("last_scan", SLOTS)
                q2 = st.v(lambda e: e.tensor_scalar(lst[:, :], ed["same_next"][:, :], -1.0, 1.0, ALU.mult, ALU.add), q)
        fin = to_slots(k, st, c, ed["last"], lambda g: lst[:, g * P:(g + 1) * P], [q2, kk, y], (6, 7))
        spread = sb("flag_cols", 4 * R)
        zs = []
        for j, (n, cix) in enumerate((("pre_add", SLOTS - 1), ("suf_add", 0), ("pre_mul", SLOTS - 1), ("suf_mul", 0))):
            zs.append(st.v(lambda e, j=j, n=n, cix=cix: e.tensor_copy(
                spread[:, j * R:(j + 1) * R], ed[n][:, cix:cix + 1].to_broadcast([P, R])), (st.done["vector"], st.done["vector"].count)))
        for j in range(4):
            m = st.t(lambda e, j=j: e.transpose(k.psum[1][0:R, j * P:(j + 1) * P], spread[:, j * R:(j + 1) * R],
                                                c["ident"][:, :]), zs)
        st.v(lambda e: e.tensor_copy(ed["flags"][:, :], k.psum[1][0:R, 0:4 * P]), m)
        st.run()


def segment_reduce(k, st, c, ed, own, tag, kind, vals, after):
    C = len(vals)
    big = kind == "max"
    step = (ed["add_prev"], ed["add_next"]) if big else (ed["same_prev"], ed["same_next"])
    reach = (ed["pre_add"], ed["suf_add"]) if big else (ed["pre_mul"], ed["suf_mul"])
    op0, op1 = (ALU.add, ALU.max) if big else (ALU.mult, ALU.add)
    neutral = -BIG if big else 0.0
    outs = [[k.sb(f"{tag}_{d}{j}", SLOTS, ctx=own) for j in range(C)] for d in "fb"]
    ends = k.sb(f"{tag}_ends", 2 * C, ctx=own)
    rows = k.sb(f"{tag}_rows", 2 * P, rows=C, ctx=own)
    carry_rows = k.sb(f"{tag}_carry_rows", 2 * P + 2, rows=C, ctx=own)
    carry = k.sb(f"{tag}_carry", 2 * C, ctx=own)
    t = []
    for w in (0, 1):
        d = slice(None, None, -1) if w else slice(None)
        for j in range(C):
            q = st.v(lambda e, w=w, j=j, d=d: e.tensor_tensor_scan(outs[w][j][:, d], step[w][:, d], vals[j][:, d],
                                                                   neutral, op0, op1), after)
            cix = 0 if w else SLOTS - 1
            t.append(st.v(lambda e, w=w, j=j, cix=cix: e.tensor_copy(ends[:, w * C + j:w * C + j + 1],
                                                                     outs[w][j][:, cix:cix + 1]), q))
    ps = k.psum[0]
    for w in (0, 1):
        m = st.t(lambda e, w=w: e.transpose(ps[0:C, w * P:(w + 1) * P], ends[:, w * C:(w + 1) * C],
                                            c["ident"][:, :]), t)
    z = [st.v(lambda e: e.memset(carry_rows[:, 0:1], neutral)),
         st.v(lambda e: e.memset(carry_rows[:, 2 * P + 1:2 * P + 2], neutral)),
         st.v(lambda e: e.tensor_copy(rows[:, :], ps[0:C, 0:2 * P]), m)]
    f0 = 0 if big else 2
    z.append(st.v(lambda e: e.tensor_tensor_scan(carry_rows[:, 1:P + 1], ed["flags"][0:C, f0 * P:(f0 + 1) * P],
                                                 rows[:, 0:P], neutral, op0, op1), z))
    z.append(st.v(lambda e: e.tensor_tensor_scan(carry_rows[:, P + 1:2 * P + 1][:, ::-1],
                                                 ed["flags"][0:C, (f0 + 1) * P:(f0 + 2) * P][:, ::-1],
                                                 rows[:, P:2 * P][:, ::-1], neutral, op0, op1), z))
    st.t(lambda e: e.transpose(k.psum[1][:, 0:C], carry_rows[:, 0:P], c["ident"][0:C, 0:C]), z)
    m = st.t(lambda e: e.transpose(k.psum[1][:, C:2 * C], carry_rows[:, P + 2:2 * P + 2], c["ident"][0:C, 0:C]), z)
    cc = st.v(lambda e: e.tensor_copy(carry[:, :], k.psum[1][:, 0:2 * C]), m)
    done = []
    for j in range(C):
        both = []
        for w in (0, 1):
            both.append(st.v(lambda e, w=w, j=j: e.scalar_tensor_tensor(
                out=outs[w][j][:, :], in0=reach[w][:, :], scalar=carry[:, w * C + j:w * C + j + 1],
                in1=outs[w][j][:, :], op0=op0, op1=op1), cc))
        if not big:
            both.append(st.v(lambda e, j=j: e.tensor_tensor(outs[1][j][:, :], outs[1][j][:, :], vals[j][:, :],
                                                            ALU.subtract), both))
        done.append(st.v(lambda e, j=j: e.tensor_tensor(outs[0][j][:, :], outs[0][j][:, :], outs[1][j][:, :],
                                                        ALU.max if big else ALU.add), both))
    return outs[0], done


def rows_to_cols(k, st, c, rows, cols, after):
    ring = Ring([6, 7])
    done = []
    for lo in range(0, NB, 4):
        hi = min(lo + 4, NB)
        s, bank, free = ring.take()
        for b in range(lo, hi):
            t = st.t(lambda e, b=b, lo=lo, bank=bank: e.transpose(
                k.psum[bank][:, (b - lo) * P:(b - lo + 1) * P], rows[:, b * P:(b + 1) * P], c["ident"][:, :]),
                after, free)
        if (lo // 4) % 2:
            d = st.s(lambda e, lo=lo, hi=hi, bank=bank: e.copy(cols[:, lo * P:hi * P], k.psum[bank][:, 0:(hi - lo) * P]), t)
        else:
            d = st.v(lambda e, lo=lo, hi=hi, bank=bank: e.tensor_copy(cols[:, lo * P:hi * P],
                                                                      k.psum[bank][:, 0:(hi - lo) * P]), t)
        ring.free[s] = d
        done.append(d)
    return done


def linear_rows(k, st, cols, weight, bias_row, out, after):
    ring = Ring([4, 5])
    done = []
    for lo in range(0, NB, 4):
        hi = min(lo + 4, NB)
        s, bank, free = ring.take()
        for b in range(lo, hi):
            t = st.t(lambda e, b=b, lo=lo, bank=bank: e.matmul(
                k.psum[bank][:, (b - lo) * P:(b - lo + 1) * P], cols[:, b * P:(b + 1) * P], weight,
                start=True, stop=True), after, free)
        view = lambda x, lo=lo, hi=hi: x[:, lo * P:hi * P].rearrange("p (b f) -> p b f", f=F)
        if bias_row is None:
            d = st.s(lambda e, lo=lo, hi=hi, bank=bank: e.copy(out[:, lo * P:hi * P],
                                                               k.psum[bank][:, 0:(hi - lo) * P]), t)
        else:
            d = st.v(lambda e, lo=lo, hi=hi, bank=bank, view=view: e.tensor_tensor(
                view(out), k.psum[bank][:, 0:(hi - lo) * P].rearrange("p (b f) -> p b f", f=F),
                bias_row.unsqueeze(1).to_broadcast([P, hi - lo, F]), ALU.add), t, after)
        ring.free[s] = d
        done.append(d)
    return done


def layernorm_rows(k, st, own, tag, x, out, after, gain=None, shift=None):
    x3, o3 = blocks3(x), blocks3(out)
    s = k.sb(tag + "_stat", 3 * NB, ctx=own)
    v = st.v(lambda e: e.tensor_reduce(s[:, 0:NB], x3, AX_X, ALU.add), after)
    v = st.v(lambda e: e.tensor_scalar(s[:, 0:NB], s[:, 0:NB], 1.0 / F, None, ALU.mult), v)
    v = st.v(lambda e: e.tensor_tensor(x3, x3, over(s[:, 0:NB], F), ALU.subtract), v)
    v = st.s(lambda e: e.square(out[:, :], x[:, :]), v, after)
    v = st.v(lambda e: e.tensor_reduce(s[:, NB:2 * NB], o3, AX_X, ALU.add), v)
    v = st.v(lambda e: e.tensor_scalar(s[:, NB:2 * NB], s[:, NB:2 * NB], 1.0 / F, LN_EPS, ALU.mult, ALU.add), v)
    v = st.s(lambda e: e.sqrt(s[:, 2 * NB:3 * NB], s[:, NB:2 * NB]), v)
    v = st.v(lambda e: e.reciprocal(s[:, 2 * NB:3 * NB], s[:, 2 * NB:3 * NB]), v)
    v = st.v(lambda e: e.tensor_tensor(o3, x3, over(s[:, 2 * NB:3 * NB], F), ALU.mult), v)
    if gain is not None:
        v = st.v(lambda e: e.tensor_tensor(o3, o3, gain.unsqueeze(1).to_broadcast([P, NB, F]), ALU.mult), v)
        v = st.v(lambda e: e.tensor_tensor(o3, o3, shift.unsqueeze(1).to_broadcast([P, NB, F]), ALU.add), v)
    return v


def store_rows(k, st, engine, table, rows, sem, after, width=F):
    return st.dma(engine, lambda e: e.dma_start(table[:, :].rearrange("(b p) f -> p b f", p=P),
                                                rows[:, :].rearrange("p (b f) -> p b f", f=width)), sem, after)


def broadcast_row(vec):
    return vec.partition_broadcast(P)


def aggregate_rows(k, c, ed, name, table, acc, width):
    with ExitStack() as own:
        st = k.stage(name)
        NG, NS = 8, 4
        gathered = Ring([k.sb(f"{name}_rows{j}", width, ctx=own) for j in range(NG)])
        hot = Ring([k.sb(f"{name}_hot{j}", P, ctx=own) for j in range(NS)])
        bank = Ring([0, 1, 2, 3])
        zero = st.v(lambda e: e.memset(acc[:, :], 0.0))
        ones = [st.v(lambda e, j=j: e.memset(gathered.items[j][:, F:width], 1.0)) for j in range(NG)] if width > F else []
        last_add, hold, pend = zero, [], None

        def add_up(item):
            i, bk, slot, product = item
            nonlocal last_add
            if i % BATCH == 0:
                st.plain("vector", lambda e: (hold.clear(), hold.extend(k.regs(ENG.DVE, ed["acc_row"], i, BATCH,
                                                                               (NB - 1) * ROW))))
            last_add = st.v(lambda e: e.tensor_tensor(acc[:, bass.ds(hold[i % BATCH], width)],
                                                      acc[:, bass.ds(hold[i % BATCH], width)],
                                                      k.psum[bk][:, 0:width], ALU.add), product, last_add)
            bank.free[slot] = last_add

        for i in range(TILES):
            gs, rows, gfree = gathered.take()
            got = st.dma("gpsimd", lambda e, rows=rows, i=i: e.indirect_dma_start(
                rows[:, 0:F], None, table[:, :], bass.IndirectOffsetOnAxis(ap=ed["src"][:, i:i + 1], axis=0)),
                k.pool_sems[gs], gfree)
            hs, s, hfree = hot.take()
            made = st.v(lambda e, s=s, i=i: e.tensor_scalar(s[:, :], c["node_iota"][:, :], ed["local"][:, i:i + 1],
                                                            None, ALU.is_equal), hfree)
            bs, bk, bfree = bank.take()
            prod = st.t(lambda e, s=s, rows=rows, bk=bk: e.matmul(k.psum[bk][:, 0:width], s[:, :], rows[:, 0:width],
                                                                  start=True, stop=True), got, made, bfree, ones)
            gathered.free[gs] = hot.free[hs] = prod
            if pend is not None:
                add_up(pend)
            pend = (i, bk, bs, prod)
        add_up(pend)
        st.run()


def gin_layer(k, c, ed, w, x, acc, degree):
    aggregate_rows(k, c, ed, "gin_sum", w["x"], acc, F + 1)
    with ExitStack() as own:
        st = k.stage("gin_mlp")
        acc3 = blocks3(acc, ROW)
        par = k.sb("gin_par", 16, ctx=own)
        w1, w2 = k.sb("gin_w1", F, ctx=own), k.sb("gin_w2", F, ctx=own)
        loads = [(par[:, 0:1], broadcast_row(w["L0_gnn_eps"])), (par[:, 1:2], broadcast_row(w["L0_gnn_a1"])),
                 (par[:, 2:3], broadcast_row(w["L0_gnn_a2"])), (w1[:, :], w["L0_gnn_W1"]), (w2[:, :], w["L0_gnn_W2"])]
        for j, n in enumerate(("b1", "gamma1", "beta1", "b2", "gamma2", "beta2")):
            loads.append((par[:, 3 + j:4 + j], w["L0_gnn_" + n].unsqueeze(1)))
        for dst, src in loads:
            par_in = st.dma("sync", lambda e, dst=dst, src=src: e.dma_start(dst, src), k.dma_sems[8])
        st.v(lambda e: e.tensor_copy(degree[:, :], acc3[:, :, F:F + 1].rearrange("p b o -> p (b o)")))
        h, cols = k.sb("gin_h", NP, ctx=own), k.sb("gin_cols", NP, ctx=own)
        v = st.v(lambda e: e.tensor_scalar(par[:, 0:1], par[:, 0:1], 1.0, None, ALU.add), par_in)
        v = st.v(lambda e: e.scalar_tensor_tensor(out=blocks3(h), in0=blocks3(x), scalar=par[:, 0:1],
                                                  in1=acc3[:, :, 0:F], op0=ALU.mult, op1=ALU.add), v)
        ready = rows_to_cols(k, st, c, h, cols, [v])
        for layer, (wt, b0, slope) in enumerate(((w1, 3, 1), (w2, 6, 2))):
            ring, done = Ring([0, 1, 2, 3]), []
            for j in range(NP // CH):
                s, bk, free = ring.take()
                t = st.t(lambda e, j=j, bk=bk, wt=wt: e.matmul(k.psum[bk][:, 0:CH], wt[:, :],
                                                               cols[:, j * CH:(j + 1) * CH], start=True, stop=True),
                         ready, free, par_in)
                ring.free[s] = st.s(lambda e, j=j, bk=bk, b0=b0: e.activation(
                    h[:, j * CH:(j + 1) * CH], k.psum[bk][:, 0:CH], ACT.Identity, bias=par[:, b0:b0 + 1]), t)
                done.append(ring.free[s])
            q = lambda a: par[:, a:a + 1]
            v = st.v(lambda e: e.tensor_reduce(q(9), h[:, 0:N], AX_X, ALU.add), done)
            v = st.v(lambda e: e.tensor_scalar(q(9), q(9), 1.0 / N, None, ALU.mult), v)
            v = st.v(lambda e: e.tensor_scalar(h[:, :], h[:, :], q(9), None, ALU.subtract), v)
            v = st.s(lambda e: e.activation(cols[:, 0:N], h[:, 0:N], ACT.Square, accum_out=q(10)), v)
            v = st.v(lambda e: e.tensor_scalar(q(10), q(10), 1.0 / N, LN_EPS, ALU.mult, ALU.add), v)
            v = st.s(lambda e: e.sqrt(q(11), q(10)), v)
            v = st.v(lambda e: e.reciprocal(q(12), q(11)), v)
            v = st.v(lambda e, b0=b0: e.tensor_tensor(q(12), q(12), q(b0 + 1), ALU.mult), v)
            v = st.v(lambda e, b0=b0: e.tensor_scalar(h[:, :], h[:, :], q(12), q(b0 + 2), ALU.mult, ALU.add), v)
            v = st.v(lambda e, slope=slope: e.tensor_scalar(cols[:, :], h[:, :], 0.0, q(slope), ALU.min, ALU.mult), v)
            v = st.v(lambda e: e.scalar_tensor_tensor(out=cols[:, :], in0=h[:, :], scalar=0.0, in1=cols[:, :],
                                                      op0=ALU.max, op1=ALU.add), v)
            ready = [v]
        done = rows_to_cols(k, st, c, cols, h, ready)
        v = st.v(lambda e: e.tensor_tensor(h[:, :], h[:, :], x[:, :], ALU.add), done)
        layernorm_rows(k, st, own, "ln0", h, x, [v])
        st.run()


def gat_layer(k, c, ed, w, layer, h_in, acc, table, spill, combine):
    name = f"gat{layer}"
    with ExitStack() as own:
        g = h_in
        node = k.sb(name + "_node", 10 * NB, ctx=own)
        nd = lambda j: node[:, j * NB:(j + 1) * NB]
        sp, dp, sdp = (k.sb(f"{name}_{n}", IT, ctx=own) for n in ("src_term", "dst_term", "self_term"))
        bias = k.sb(name + "_bias", F, ctx=own)
        with ExitStack() as pre:
            st = k.stage(name + "_nodes")
            cols = k.sb(name + "_cols", NP, ctx=pre)
            wt = k.sb(name + "_w", F, ctx=pre)
            att = k.sb(name + "_att", 2 * F, ctx=pre)
            for dst, src in ((wt[:, :], w["L1_gnn_lyr_W"][layer]), (att[:, 0:F], broadcast_row(w["L1_gnn_att_src"][layer])),
                             (att[:, F:2 * F], broadcast_row(w["L1_gnn_att_dst"][layer])),
                             (bias[:, :], broadcast_row(w["L1_gnn_lyr_bias"][layer]))):
                got = st.dma("sync", lambda e, dst=dst, src=src: e.dma_start(dst, src), k.dma_sems[8])
            ready = rows_to_cols(k, st, c, h_in, cols, [])
            done = linear_rows(k, st, cols, wt[:, :], None, g, [ready, got])
            v = done
            for j in (0, 1):
                v = st.v(lambda e, j=j: e.tensor_tensor(blocks3(cols), blocks3(g), att[:, j * F:(j + 1) * F].unsqueeze(
                    1).to_broadcast([P, NB, F]), ALU.mult), v)
                v = st.v(lambda e, j=j: e.tensor_reduce(nd(j), blocks3(cols), AX_X, ALU.add), v)
            tail = k.sb(name + "_tail", 2 * NB, ctx=pre)
            t3 = tail[:, :].rearrange("p (b o) -> p b o", o=2)
            a = st.v(lambda e: e.memset(tail[:, :], 1.0))
            a = st.v(lambda e: e.tensor_copy(t3[:, :, 1], nd(0)), a, v)
            tv = table[:, :].rearrange("(b p) f -> p b f", p=P)
            o1 = st.dma("sync", lambda e: e.dma_start(tv[:, :, 0:F], blocks3(g)), k.dma_sems[9], done)
            o2 = st.dma("sync", lambda e: e.dma_start(tv[:, :, F:ROW], t3), k.dma_sems[9], a)
            st.wait("sync", o1, o2)
            st.run()

        with ExitStack() as mid:
            st = k.stage(name + "_gather")
            dB, sB = acc, k.sb(name + "_sB", NP, ctx=mid)
            ring, done = Ring([4, 5, 6, 7]), []
            for j, out in ((1, dB), (0, sB)):
                for lo in range(0, NB, 4):
                    hi = min(lo + 4, NB)
                    s, bk, free = ring.take()
                    for b in range(lo, hi):
                        t = st.t(lambda e, b=b, lo=lo, bk=bk, j=j: e.matmul(
                            k.psum[bk][:, (b - lo) * P:(b - lo + 1) * P], nd(j)[:, b:b + 1].to_broadcast([P, P]),
                            c["ident"][:, :], start=True, stop=True), free)
                    ring.free[s] = st.s(lambda e, lo=lo, hi=hi, bk=bk, out=out: e.copy(
                        out[:, lo * P:hi * P], k.psum[bk][:, 0:(hi - lo) * P]), t)
                    done.append(ring.free[s])
            rows = Ring([k.sb(f"{name}_in{j}", BATCH * ROW, ctx=mid) for j in range(3)])
            junk = [k.sb(f"{name}_pick{j}", P, ctx=mid) for j in range(4)]
            jt = [None] * 4
            tail_cols = [st.v(lambda e, t=t: e.memset(t[:, TILES:IT], 0.0)) for t in (sp, dp, sdp)]
            spilled = []
            for j in range(0, TILES, BATCH):
                s, buf, free = rows.take()
                for n in range(BATCH):
                    got = st.dma("gpsimd", lambda e, buf=buf, n=n, j=j: e.indirect_dma_start(
                        buf[:, n * ROW:(n + 1) * ROW], None, table[:, :],
                        bass.IndirectOffsetOnAxis(ap=ed["src"][:, j + n:j + n + 1], axis=0)), k.pool_sems[s], free)
                sc = st.s(lambda e, buf=buf, j=j: e.copy(sp[:, j:j + BATCH].unsqueeze(2), buf[:, :].rearrange(
                    "p (t f) -> p t f", f=ROW)[:, :, ROW - 1:ROW]), got)
                out = st.dma("sync", lambda e, buf=buf, j=j: e.dma_start(spill[:, j * ROW:(j + BATCH) * ROW],
                                                                         buf[:, :]), k.dma_sems[3 + s], got)
                rows.free[s] = [sc, out]
                spilled.append(out)
                hold = []
                st.plain("vector", lambda e, j=j, hold=hold: hold.extend(
                    k.regs(ENG.DVE, ed["blk_row"], j, BATCH, (NB - 1) * P)))
                for n in range(BATCH):
                    for a, (tabl, out_) in enumerate(((dB, dp), (sB, sdp))):
                        z = (2 * n + a) % 4
                        jt[z] = st.v(lambda e, n=n, j=j, z=z, tabl=tabl, out_=out_, hold=hold: e.scalar_tensor_tensor(
                            out=junk[z][:, :], in0=c["node_iota"][:, :], scalar=ed["local"][:, j + n:j + n + 1],
                            in1=tabl[:, bass.ds(hold[n], P)], op0=ALU.is_equal, op1=ALU.mult,
                            accum_out=out_[:, j + n:j + n + 1]), jt[z], done)
            st.wait("sync", spilled[-3:])
            st.run()

        with ExitStack() as soft:
            st = k.stage(name + "_softmax")
            s_scan = k.sb(name + "_s_scan", SLOTS, ctx=soft)
            a = to_scan(k, st, c, s_scan, sp[:, :], [], (2, 3))
            (mx,), done = segment_reduce(k, st, c, ed, soft, name + "_mx", "max", [s_scan], [a])
            mxp = k.sb(name + "_mxp", IT, ctx=soft)
            b_ = to_slots(k, st, c, mxp, lambda g_: mx[:, g_ * P:(g_ + 1) * P], done, (4, 5))
            v = st.v(lambda e: e.tensor_tensor(mxp[:, :], mxp[:, :], sdp[:, :], ALU.max), b_)

            def leaky_sum(dst, a_, b_, tickets):
                q = st.v(lambda e: e.tensor_tensor(dst, a_, b_, ALU.add), tickets)
                return st.v(lambda e: e.scalar_tensor_tensor(out=dst, in0=dst, scalar=0.2, in1=dst, op0=ALU.mult,
                                                             op1=ALU.max), q)
            v = leaky_sum(mxp[:, :], mxp[:, :], dp[:, :], v)
            u = leaky_sum(sp[:, :], sp[:, :], dp[:, :], [a])
            u = st.v(lambda e: e.tensor_tensor(sp[:, :], sp[:, :], mxp[:, :], ALU.subtract), u, v)
            u = st.v(lambda e: e.tensor_scalar(sp[:, :], sp[:, :], 0.0, None, ALU.min), u)
            u = st.s(lambda e: e.activation(sp[:, :], sp[:, :], ACT.Exp), u)
            st.v(lambda e: e.tensor_tensor(dp[:, :], mxp[:, :], ed["last"][:, :], ALU.mult), v, u)
            st.run()

        with ExitStack() as late:
            st = k.stage(name + "_sum")
            rows = Ring([k.sb(f"{name}_back{j}", BATCH * ROW, ctx=late) for j in range(3)])
            hot = Ring([k.sb(f"{name}_hot{j}", P, ctx=late) for j in range(4)])
            hotw = Ring([k.sb(f"{name}_hotw{j}", P, ctx=late) for j in range(4)])
            bank = Ring([0, 1, 2, 3])
            last_add = st.v(lambda e: e.memset(acc[:, :], 0.0))
            hold, pend = [], None

            def add_up(item):
                nonlocal last_add
                i, bk, slot, product = item
                if i % BATCH == 0:
                    st.plain("vector", lambda e: (hold.clear(), hold.extend(k.regs(ENG.DVE, ed["acc_row"], i, BATCH,
                                                                                   (NB - 1) * ROW))))
                last_add = st.v(lambda e: e.tensor_tensor(acc[:, bass.ds(hold[i % BATCH], ROW)],
                                                          acc[:, bass.ds(hold[i % BATCH], ROW)],
                                                          k.psum[bk][:, 0:ROW], ALU.add), product, last_add)
                bank.free[slot] = last_add

            for j in range(0, TILES, BATCH):
                s, buf, free = rows.take()
                got = st.dma("sync", lambda e, buf=buf, j=j: e.dma_start(buf[:, :], spill[:, j * ROW:(j + BATCH) * ROW]),
                             k.dma_sems[s], free)
                for n in range(BATCH):
                    i = j + n
                    hs, ht, hfree = hot.take()
                    made = st.v(lambda e, ht=ht, i=i: e.tensor_scalar(ht[:, :], c["node_iota"][:, :],
                                                                      ed["local"][:, i:i + 1], None, ALU.is_equal), hfree)
                    ws, hw, wfree = hotw.take()
                    scaled = st.s(lambda e, ht=ht, hw=hw, i=i: e.mul(hw[:, :], ht[:, :], sp[:, i:i + 1]), made, wfree)
                    bs, bk, bfree = bank.take()
                    m1 = st.t(lambda e, ht=ht, i=i, bk=bk: e.matmul(k.psum[bk][:, F + 1:F + 2], ht[:, :], dp[:, i:i + 1],
                                                                   start=True, stop=True), made, bfree)
                    m2 = st.t(lambda e, hw=hw, n=n, buf=buf, bk=bk: e.matmul(
                        k.psum[bk][:, 0:F + 1], hw[:, :], buf[:, n * ROW:n * ROW + F + 1], start=True, stop=True),
                        scaled, got)
                    hot.free[hs] = [m1, scaled]
                    hotw.free[ws] = m2
                    if pend is not None:
                        add_up(pend)
                    pend = (i, bk, bs, m2)
                rows.free[s] = m2
            add_up(pend)
            st.run()

        st = k.stage(name + "_out")
        acc3 = blocks3(acc, ROW)
        es, has, m = nd(2), nd(3), nd(4)
        v = st.v(lambda e: e.tensor_tensor(es, nd(0), nd(1), ALU.add))
        v = st.v(lambda e: e.scalar_tensor_tensor(out=es, in0=es, scalar=0.2, in1=es, op0=ALU.mult, op1=ALU.max), v)
        v = st.v(lambda e: e.tensor_scalar(has, ed["degree"][:, :], 0.0, None, ALU.is_equal), v)
        v = st.v(lambda e: e.tensor_tensor(m, has, es, ALU.mult), v)
        v = st.v(lambda e: e.tensor_tensor(m, m, acc3[:, :, F + 1], ALU.add), v)
        v = st.v(lambda e: e.tensor_tensor(es, es, m, ALU.subtract), v)
        v = st.s(lambda e: e.activation(nd(5), es, ACT.Exp), v)
        v = st.v(lambda e: e.tensor_tensor(nd(6), acc3[:, :, F], nd(5), ALU.add), v)
        v = st.v(lambda e: e.reciprocal(nd(7), nd(6)), v)
        v = st.v(lambda e: e.tensor_tensor(blocks3(g), blocks3(g), over(nd(5), F), ALU.mult), v)
        v = st.v(lambda e: e.tensor_tensor(blocks3(g), blocks3(g), acc3[:, :, 0:F], ALU.add), v)
        v = st.v(lambda e: e.tensor_tensor(blocks3(g), blocks3(g), over(nd(7), F), ALU.mult), v)
        v = st.v(lambda e: e.tensor_tensor(blocks3(g), blocks3(g), bias[:, :].unsqueeze(1).to_broadcast([P, NB, F]),
                                           ALU.add), v)
        combine(st, own, g, [v])
        st.run()


def relational_layer(k, c, ed, w, x, acc, tabs):
    left, right, attr = tabs
    with ExitStack() as own:
        idx_l, idx_r = k.sb("idx_l", IT, I32, ctx=own), k.sb("idx_r", IT, I32, ctx=own)
        score = k.sb("score", IT * H, ctx=own)
        wpack, attp = k.sb("edge_w", HC, ctx=own), k.sb("att_w", HC, ctx=own)
        gate = k.sb("gate", 8 + 4 * R, ctx=own)
        b_row = k.sb("rel_bias", R * F, ctx=own)
        with ExitStack() as pre:
            st = k.stage("rel_tables")
            cols = acc
            wl, bl = k.sb("rel_wl", R * HC, ctx=pre), k.sb("rel_bl", R * HC, ctx=pre)
            rel = k.sb("rel_emb", R, rows=DR, ctx=pre)
            wrel = k.sb("rel_we", R * HC, rows=DR, ctx=pre)
            ready = rows_to_cols(k, st, c, x, cols, [])
            tmpi = k.sb("rel_idx", IT, ctx=pre)
            for out, base in ((idx_l, "src"), (idx_r, "dst")):
                v = st.v(lambda e, base=base: e.tensor_copy(tmpi[:, :], ed[base][:, :]), (st.done["vector"], st.done["vector"].count))
                v = st.v(lambda e: e.scalar_tensor_tensor(out=tmpi[:, :], in0=tmpi[:, :], scalar=float(R),
                                                          in1=ed["type"][:, :], op0=ALU.mult, op1=ALU.add), v)
                v = st.v(lambda e, out=out: e.tensor_tensor(out[:, :], tmpi[:, :], ed["valid"][:, :], ALU.mult), v)
            for r in range(R):
                st.dma("sync", lambda e, r=r: e.dma_start(wpack[r * DE:(r + 1) * DE, :], w["L2_gnn_W_e"][r, 0:DE, :]), k.dma_sems[8])
                st.dma("sync", lambda e, r=r: e.dma_start(wrel[:, r * HC:(r + 1) * HC], w["L2_gnn_W_e"][r, DE:DE + DR, :]), k.dma_sems[8])
                st.dma("sync", lambda e, r=r: e.dma_start(rel[:, r:r + 1], w["L2_gnn_rel_emb"][r].unsqueeze(1)), k.dma_sems[8])
            st.dma("sync", lambda e: e.dma_start(attp[R * DE:R * DE + R, :], w["L2_gnn_att"].rearrange("r h c -> r (h c)")), k.dma_sems[8])
            st.dma("sync", lambda e: e.dma_start(b_row[:, :], broadcast_row(w["L2_gnn_bias"].rearrange("r c -> (r c)"))), k.dma_sems[8])
            gl = st.dma("sync", lambda e: e.dma_start(gate[:, 0:R], broadcast_row(w["L2_gnn_gate"])), k.dma_sems[8])
            emb = k.sb("rel_row", R * HC, rows=1, ctx=pre)
            for r in range(R):
                m = st.t(lambda e, r=r: e.matmul(k.psum[0][0:1, 0:HC], rel[:, r:r + 1], wrel[:, r * HC:(r + 1) * HC],
                                                 start=True, stop=True), gl, v)
                v = st.v(lambda e, r=r: e.tensor_copy(emb[:, r * HC:(r + 1) * HC], k.psum[0][0:1, 0:HC]), m)
            for r in range(R):
                st.dma("sync", lambda e, r=r: e.dma_start(wpack[R * DE + r:R * DE + r + 1, :], emb[:, r * HC:(r + 1) * HC]),
                       k.dma_sems[9], v)
            st.wait("sync", (k.dma_sems[9], k.dma_sems[9].count))
            gq = lambda a, n=1: gate[:, a:a + n]
            v = st.v(lambda e: e.tensor_reduce(gq(R), gq(0, R), AX_X, ALU.max), gl)
            v = st.v(lambda e: e.tensor_scalar(gq(0, R), gq(0, R), gq(R), None, ALU.subtract), v)
            v = st.s(lambda e: e.activation(gq(8, R), gq(0, R), ACT.Exp), v)
            v = st.v(lambda e: e.tensor_reduce(gq(R + 1), gq(8, R), AX_X, ALU.add), v)
            v = st.v(lambda e: e.reciprocal(gq(R + 2), gq(R + 1)), v)
            v = st.v(lambda e: e.tensor_scalar(gq(8, R), gq(8, R), gq(R + 2), None, ALU.mult), v)
            st.v(lambda e: e.tensor_scalar(gq(8 + R, R), gq(8, R), 1.0 / H, None, ALU.mult), v)
            out_ring = Ring([k.sb(f"rel_out{j}", R * HC, ctx=pre) for j in range(3)])
            bank = Ring([0, 1, 2, 3])
            busy, side_done = v, None
            for side, (wn, bn, tab) in enumerate((("L2_gnn_W_l", "L2_gnn_b_l", left), ("L2_gnn_W_r", "L2_gnn_b_r", right))):
                for r in range(R):
                    st.dma("scalar", lambda e, r=r, wn=wn: e.dma_start(wl[:, r * HC:(r + 1) * HC], w[wn][r]), k.dma_sems[10],
                           side_done)
                wgot = st.dma("scalar", lambda e, bn=bn: e.dma_start(bl[:, :], broadcast_row(w[bn].rearrange("r f -> (r f)"))),
                              k.dma_sems[10], side_done)
                tview = tab[:, :].rearrange("(b p r) f -> b p (r f)", p=P, r=R)
                for b in range(NB):
                    os_, ob, ofree = out_ring.take()
                    parts = []
                    for r in range(R):
                        bs, bk, bfree = bank.take()
                        m = st.t(lambda e, b=b, r=r, bk=bk: e.matmul(k.psum[bk][:, 0:HC], cols[:, b * P:(b + 1) * P],
                                                                     wl[:, r * HC:(r + 1) * HC], start=True, stop=True),
                                 ready, wgot, bfree, busy)
                        a = st.v(lambda e, r=r, bk=bk, ob=ob: e.tensor_tensor(
                            ob[:, r * HC:(r + 1) * HC], k.psum[bk][:, 0:HC], bl[:, r * HC:(r + 1) * HC], ALU.add),
                            m, wgot, ofree)
                        bank.free[bs] = a
                        parts.append(a)
                    out_ring.free[os_] = st.dma("sync", lambda e, b=b, ob=ob, tview=tview: e.dma_start(tview[b], ob[:, :]),
                                                k.dma_sems[11 + os_], parts)
                side_done = parts
            st.wait("sync", [(k.dma_sems[11 + j], k.dma_sems[11 + j].count) for j in range(3)])
            st.run()

        with ExitStack() as mid:
            st = k.stage("rel_scores")
            NG = 4
            KA = R * DE + R
            type_of_row = k.sb("type_of_row", 1, ctx=mid)
            tor_i = k.sb("type_of_row_i", 2, I32, ctx=mid)
            gl_ = Ring([k.sb(f"xl{j}", HC, ctx=mid) for j in range(NG)])
            gr_ = Ring([k.sb(f"xr{j}", HC, ctx=mid) for j in range(NG)])
            feats = Ring([k.sb(f"feat{j}", P, ctx=mid) for j in range(NG)])
            types = Ring([k.sb(f"types{j}", P, I32, ctx=mid) for j in range(NG)])
            masked = Ring([k.sb(f"masked{j}", P, ctx=mid) for j in range(2)])
            pre_act = Ring([k.sb(f"pre_act{j}", HC, ctx=mid) for j in range(3)])
            act_out = Ring([k.sb(f"act_out{j}", HC, ctx=mid) for j in range(2)])
            bank_e, bank_a = Ring([0, 1]), Ring([2, 3])
            a = st.g(lambda e: e.iota(tor_i[:, 0:1], pattern=[[0, 1]], base=0, channel_multiplier=1))
            b1 = st.v(lambda e: e.tensor_scalar(tor_i[0:R * DE, 1:2], tor_i[0:R * DE, 0:1], 4, None, ALU.arith_shift_right), a)
            b2 = st.v(lambda e: e.tensor_scalar(tor_i[R * DE:KA, 1:2], tor_i[R * DE:KA, 0:1], 3, None, ALU.bitwise_and), a)
            tor = st.v(lambda e: e.tensor_copy(type_of_row[0:KA, :], tor_i[0:KA, 1:2]), b1, b2)
            tor = [tor] + [st.v(lambda e, f=f: e.memset(f[R * DE:KA, :], 1.0)) for f in feats.items]
            tor.append(st.v(lambda e: e.memset(score[:, TILES * H:IT * H], 0.0)))
            hold, waiting = [], []

            def finish(item):
                i, act, act_slot, made, bk, bslot, att_done = item
                for h in range(H):
                    d = st.v(lambda e, h=h, act=act, bk=bk, i=i: e.tensor_tensor_reduce(
                        out=act[:, h * F:(h + 1) * F], in0=act[:, h * F:(h + 1) * F],
                        in1=k.psum[bk][:, h * F:(h + 1) * F], scale=1.0, scalar=0.0, op0=ALU.mult, op1=ALU.add,
                        accum_out=score[:, i * H + h:i * H + h + 1]), made, att_done)
                act_out.free[act_slot] = d
                bank_a.free[bslot] = d

            for i in range(TILES):
                s, xl, free = gl_.take()
                _, xr, _ = gr_.take()
                _, ft, _ = feats.take()
                _, ty, _ = types.take()
                got_l = st.dma("gpsimd", lambda e, xl=xl, i=i: e.indirect_dma_start(
                    xl[:, :], None, left[:, :], bass.IndirectOffsetOnAxis(ap=idx_l[:, i:i + 1], axis=0)), k.pool_sems[s], free)
                got_r = st.dma("gpsimd", lambda e, xr=xr, i=i: e.indirect_dma_start(
                    xr[:, :], None, right[:, :], bass.IndirectOffsetOnAxis(ap=idx_r[:, i:i + 1], axis=0)), k.pool_sems[4 + s], free)
                if i % BATCH == 0:
                    hold = []
                    st.plain("sync", lambda e, i=i, hold=hold: hold.extend(k.regs(ENG.SP, ed["edge_row"], i, BATCH, E)))
                st.dma("sync", lambda e, ft=ft, i=i, hold=hold: e.dma_start(
                    ft[0:R * DE, :], attr[0][:, bass.ds(hold[i % BATCH], P)]), k.dma_sems[8 + s], free, tor)
                got_f = st.dma("sync", lambda e, ty=ty, i=i, hold=hold: e.dma_start(
                    ty[0:KA, :], attr[1][bass.ds(hold[i % BATCH], P)].partition_broadcast(KA)), k.dma_sems[8 + s], free)
                ms, mk, mfree = masked.take()
                mm = st.v(lambda e, mk=mk, ty=ty, ft=ft: e.scalar_tensor_tensor(
                    out=mk[0:KA, :], in0=ty[0:KA, :], scalar=type_of_row[0:KA, 0:1], in1=ft[0:KA, :],
                    op0=ALU.is_equal, op1=ALU.mult), got_f, mfree, tor)
                es, ek, efree = bank_e.take()
                as_, ak, afree = bank_a.take()
                t1 = st.t(lambda e, mk=mk, ek=ek: e.matmul(k.psum[ek][:, 0:HC], mk[0:KA, :], wpack[0:KA, :], start=True,
                                                           stop=True), mm, efree)
                t2 = st.t(lambda e, mk=mk, ak=ak: e.matmul(k.psum[ak][:, 0:HC], mk[R * DE:KA, :], attp[R * DE:KA, :],
                                                           start=True, stop=True), afree)
                masked.free[ms] = t2
                ps_, pa, pfree = pre_act.take()
                q1 = st.v(lambda e, pa=pa, xl=xl, xr=xr: e.tensor_tensor(pa[:, :], xl[:, :], xr[:, :], ALU.add),
                          got_l, got_r, pfree)
                if len(waiting) == 1:
                    finish(waiting.pop(0))
                q2 = st.v(lambda e, pa=pa, ek=ek: e.tensor_tensor(pa[:, :], pa[:, :], k.psum[ek][:, 0:HC], ALU.add), q1, t1)
                bank_e.free[es] = q2
                gl_.free[s] = [q1, mm]
                os_, oa, ofree = act_out.take()
                la = st.v(lambda e, pa=pa, oa=oa: e.scalar_tensor_tensor(out=oa[:, :], in0=pa[:, :], scalar=0.2,
                                                                         in1=pa[:, :], op0=ALU.mult, op1=ALU.max), q2, ofree)
                pre_act.free[ps_] = la
                waiting.append((i, oa, os_, la, ak, as_, t2))
            finish(waiting.pop(0))
            st.run()

        for h in range(H):
            with ExitStack() as soft:
                st = k.stage(f"rel_soft{h}")
                sc = k.sb("sc_scan", SLOTS, ctx=soft)
                sview = score[:, :].rearrange("q (i h) -> q i h", h=H)[:, :, h]
                a = to_scan(k, st, c, sc, sview, [], (2, 3))
                chans = [acc[:, r * SLOTS:(r + 1) * SLOTS] for r in range(R)]
                hot = [k.sb(f"is_type{r}", SLOTS, ctx=soft) for r in range(R)]
                pick = k.sb("picked", SLOTS, ctx=soft)
                t1 = []
                for r in range(R):
                    q = st.v(lambda e, r=r: e.tensor_scalar(hot[r][:, :], ed["type_scan"][:, :], float(r), None, ALU.is_equal))
                    z = st.v(lambda e, r=r: e.tensor_scalar(chans[r][:, :], hot[r][:, :], -1.0, BIG, ALU.add, ALU.mult), q)
                    z2 = st.v(lambda e, r=r: e.tensor_tensor(pick[:, :], hot[r][:, :], sc[:, :], ALU.mult), q, a, t1)
                    t1.append(st.v(lambda e, r=r: e.tensor_tensor(chans[r][:, :], chans[r][:, :], pick[:, :], ALU.add), z, z2))

                def of_own_type(outs, done):
                    v = st.v(lambda e: e.tensor_tensor(pick[:, :], hot[0][:, :], outs[0][:, :], ALU.mult), done)
                    for r in range(1, R):
                        u = st.v(lambda e, r=r: e.tensor_tensor(outs[r][:, :], hot[r][:, :], outs[r][:, :], ALU.mult), done)
                        v = st.v(lambda e, r=r: e.tensor_tensor(pick[:, :], pick[:, :], outs[r][:, :], ALU.add), u, v)
                    return v
                with ExitStack() as part:
                    outs, done = segment_reduce(k, st, c, ed, part, "rmx", "max", chans, t1)
                    v = of_own_type(outs, done)
                    v = st.v(lambda e: e.tensor_tensor(sc[:, :], sc[:, :], pick[:, :], ALU.subtract), v)
                    v = st.s(lambda e: e.activation(sc[:, :], sc[:, :], ACT.Exp), v)
                    t2 = [st.v(lambda e, r=r: e.tensor_tensor(chans[r][:, :], hot[r][:, :], sc[:, :], ALU.mult), v)
                          for r in range(R)]
                    st.run()
                    st = k.stage(f"rel_den{h}")
                with ExitStack() as part:
                    outs, done = segment_reduce(k, st, c, ed, part, "rsm", "sum", chans, [])
                    v = of_own_type(outs, done)
                    v = st.v(lambda e: e.reciprocal(pick[:, :], pick[:, :]), v)
                    v = st.v(lambda e: e.tensor_tensor(sc[:, :], sc[:, :], pick[:, :], ALU.mult), v)
                    u = st.v(lambda e: e.tensor_scalar(pick[:, :], hot[0][:, :], gate[:, 8 + R:9 + R], None, ALU.mult), v)
                    for r in range(1, R):
                        u = st.v(lambda e, r=r: e.scalar_tensor_tensor(
                            out=pick[:, :], in0=hot[r][:, :], scalar=gate[:, 8 + R + r:9 + R + r], in1=pick[:, :],
                            op0=ALU.mult, op1=ALU.add), u)
                    v = st.v(lambda e: e.tensor_tensor(sc[:, :], sc[:, :], pick[:, :], ALU.mult), u)
                    out = k.sb("w_slots", IT, ctx=part)
                    b_ = to_slots(k, st, c, out, lambda g: sc[:, g * P:(g + 1) * P], [v], (4, 5))
                    st.v(lambda e: e.tensor_copy(sview, out[:, :]), b_)
                    st.run()

        with ExitStack() as late:
            st = k.stage("rel_sum")
            NG = 6
            rows = Ring([k.sb(f"msg{j}", HC, ctx=late) for j in range(NG)])
            hot = Ring([k.sb(f"rhot{j}", P, ctx=late) for j in range(3)])
            hotw = Ring([k.sb(f"rhotw{j}", H * P, ctx=late) for j in range(3)])
            bank = Ring([0, 1, 2, 3])
            last_add = st.v(lambda e: e.memset(acc[:, :], 0.0))
            holds, pend = [], None

            def add_up(item):
                nonlocal last_add
                i, bk, slot, product = item
                if i % BATCH == 0:
                    st.plain("vector", lambda e: (holds.clear(), holds.extend(k.regs(ENG.DVE, ed["acc_row"], i, BATCH,
                                                                                     (NB - 1) * ROW))))
                last_add = st.v(lambda e: e.tensor_tensor(acc[:, bass.ds(holds[i % BATCH], F)],
                                                          acc[:, bass.ds(holds[i % BATCH], F)],
                                                          k.psum[bk][:, 0:F], ALU.add), product, last_add)
                bank.free[slot] = last_add

            for i in range(TILES):
                s, xl, free = rows.take()
                got = st.dma("gpsimd", lambda e, xl=xl, i=i: e.indirect_dma_start(
                    xl[:, :], None, left[:, :], bass.IndirectOffsetOnAxis(ap=idx_l[:, i:i + 1], axis=0)), k.pool_sems[s], free)
                hs, ht, hfree = hot.take()
                made = st.v(lambda e, ht=ht, i=i: e.tensor_scalar(ht[:, :], c["node_iota"][:, :], ed["local"][:, i:i + 1],
                                                                  None, ALU.is_equal), hfree)
                ws, hw, wfree = hotw.take()
                scaled = []
                for h in range(H):
                    if h < 2:
                        scaled.append(st.v(lambda e, hw=hw, h=h, i=i: e.tensor_scalar(
                            hw[:, h * P:(h + 1) * P], c["node_iota"][:, :], ed["local"][:, i:i + 1],
                            score[:, i * H + h:i * H + h + 1], ALU.is_equal, ALU.mult), wfree))
                    else:
                        scaled.append(st.s(lambda e, ht=ht, hw=hw, h=h, i=i: e.mul(
                            hw[:, h * P:(h + 1) * P], ht[:, :], score[:, i * H + h:i * H + h + 1]), made, wfree))
                bs, bk, bfree = bank.take()
                for h in range(H):
                    m = st.t(lambda e, hw=hw, h=h, xl=xl, bk=bk: e.matmul(
                        k.psum[bk][:, 0:F], hw[:, h * P:(h + 1) * P], xl[:, h * F:(h + 1) * F], start=(h == 0),
                        stop=(h == H - 1)), scaled[h], got, bfree)
                hot.free[hs] = scaled[2:]
                hotw.free[ws] = rows.free[s] = m
                if pend is not None:
                    add_up(pend)
                pend = (i, bk, bs, m)
            add_up(pend)
            st.run()

        with ExitStack() as tail:
            st = k.stage("rel_ffn")
            D2 = 2 * F
            par = k.sb("ffn_par", 2, ctx=tail)
            vec = k.sb("ffn_vec", 6 * F, ctx=tail)
            wf1, wf2 = k.sb("ffn_w1", D2, ctx=tail), k.sb("ffn_w2", 2 * F, ctx=tail)
            h1, cols = acc[:, 0:NP], k.sb("ffn_cols", NP, ctx=tail)
            z_ring = Ring([k.sb(f"ffn_z{j}", 8 * P, ctx=tail) for j in range(2)])
            for dst, src in ((wf1[:, :], w["L2_gnn_Wf1"]), (wf2[:, 0:F], w["L2_gnn_Wf2"][0:F, :]),
                             (wf2[:, F:D2], w["L2_gnn_Wf2"][F:D2, :]),
                             (par[:, 0:1], w["L2_gnn_bf1"][0:F].unsqueeze(1)), (par[:, 1:2], w["L2_gnn_bf1"][F:D2].unsqueeze(1)),
                             (vec[:, 0:F], broadcast_row(w["L2_gnn_g1"])), (vec[:, F:2 * F], broadcast_row(w["L2_gnn_bt1"])),
                             (vec[:, 2 * F:3 * F], broadcast_row(w["L2_gnn_g2"])), (vec[:, 3 * F:4 * F], broadcast_row(w["L2_gnn_bt2"])),
                             (vec[:, 4 * F:5 * F], broadcast_row(w["L2_gnn_bf2"]))):
                got = st.dma("sync", lambda e, dst=dst, src=src: e.dma_start(dst, src), k.dma_sems[8])
            brow = vec[:, 5 * F:6 * F]
            v = st.v(lambda e: e.tensor_scalar(brow, b_row[:, 0:F], gate[:, 8:9], None, ALU.mult))
            for r in range(1, R):
                v = st.v(lambda e, r=r: e.scalar_tensor_tensor(out=brow, in0=b_row[:, r * F:(r + 1) * F],
                                                               scalar=gate[:, 8 + r:9 + r], in1=brow, op0=ALU.mult,
                                                               op1=ALU.add), v)
            acc3 = blocks3(acc, ROW)
            v = st.v(lambda e: e.tensor_tensor(blocks3(cols), acc3[:, :, 0:F], brow.unsqueeze(1).to_broadcast([P, NB, F]),
                                               ALU.add), v)
            v = st.v(lambda e: e.tensor_tensor(cols[:, :], cols[:, :], x[:, :], ALU.add), v)
            v = layernorm_rows(k, st, tail, "ln_r1", cols, h1, [v, got], vec[:, 0:F], vec[:, F:2 * F])
            ready = rows_to_cols(k, st, c, h1, cols, [v])
            bank_z, bank_o, done = Ring([0, 1, 2, 3]), Ring([4, 5]), []
            for lo in range(0, NB, 4):
                hi = min(lo + 4, NB)
                wide = (hi - lo) * P
                zslot, z, zfree = z_ring.take()
                zs = []
                for m_ in (0, 1):
                    s, bk, free = bank_z.take()
                    t = st.t(lambda e, lo=lo, bk=bk, m_=m_, wide=wide: e.matmul(
                        k.psum[bk][:, 0:wide], wf1[:, m_ * F:(m_ + 1) * F], cols[:, lo * P:lo * P + wide],
                        start=True, stop=True), ready, free, got)
                    bank_z.free[s] = st.s(lambda e, bk=bk, m_=m_, z=z, wide=wide: e.activation(
                        z[:, m_ * 4 * P:m_ * 4 * P + wide], k.psum[bk][:, 0:wide], ACT.Silu, bias=par[:, m_:m_ + 1]),
                        t, zfree)
                    zs.append(bank_z.free[s])
                s, bk, free = bank_o.take()
                for b in range(lo, hi):
                    for m_ in (0, 1):
                        at = m_ * 4 * P + (b - lo) * P
                        t = st.t(lambda e, b=b, lo=lo, bk=bk, m_=m_, z=z, at=at: e.matmul(
                            k.psum[bk][:, (b - lo) * P:(b - lo + 1) * P], z[:, at:at + P],
                            wf2[:, m_ * F:(m_ + 1) * F], start=(m_ == 0), stop=(m_ == 1)), zs, free)
                z_ring.free[zslot] = t
                q = st.v(lambda e, lo=lo, hi=hi, bk=bk: e.tensor_tensor(
                    cols[:, lo * P:hi * P].rearrange("p (b f) -> p b f", f=F),
                    k.psum[bk][:, 0:(hi - lo) * P].rearrange("p (b f) -> p b f", f=F),
                    vec[:, 4 * F:5 * F].unsqueeze(1).to_broadcast([P, hi - lo, F]), ALU.add), t)
                bank_o.free[s] = q
                done.append(st.v(lambda e, lo=lo, hi=hi: e.tensor_tensor(
                    cols[:, lo * P:hi * P], cols[:, lo * P:hi * P], h1[:, lo * P:hi * P], ALU.add), q))
            v = layernorm_rows(k, st, tail, "ln_r2", cols, h1, done, vec[:, 2 * F:3 * F], vec[:, 3 * F:4 * F])
            v = st.v(lambda e: e.tensor_tensor(h1[:, :], h1[:, :], x[:, :], ALU.add), v)
            layernorm_rows(k, st, tail, "ln2", h1, x, [v])
            st.run()


def gcn_layer(k, c, ed, w, x, acc, table, out):
    with ExitStack() as own:
        h = k.sb("gcn_h", NP, ctx=own)
        dinv = k.sb("gcn_dinv", 2 * NB, ctx=own)
        bias = k.sb("gcn_bias", F, ctx=own)
        with ExitStack() as pre:
            st = k.stage("gcn_nodes")
            cols, wt = k.sb("gcn_cols", NP, ctx=pre), k.sb("gcn_w", F, ctx=pre)
            st.dma("sync", lambda e: e.dma_start(bias[:, :], broadcast_row(w["L3_gnn_b"])), k.dma_sems[8])
            got = st.dma("sync", lambda e: e.dma_start(wt[:, :], w["L3_gnn_W"]), k.dma_sems[8])
            v = st.v(lambda e: e.tensor_scalar(dinv[:, 0:NB], ed["degree"][:, :], 1.0, None, ALU.add))
            v = st.s(lambda e: e.sqrt(dinv[:, NB:2 * NB], dinv[:, 0:NB]), v)
            v = st.v(lambda e: e.reciprocal(dinv[:, 0:NB], dinv[:, NB:2 * NB]), v)
            ready = rows_to_cols(k, st, c, x, cols, [])
            done = linear_rows(k, st, cols, wt[:, :], None, h, [ready, got])
            v = st.v(lambda e: e.tensor_tensor(blocks3(h), blocks3(h), over(dinv[:, 0:NB], F), ALU.mult), v, done)
            o = store_rows(k, st, "sync", table, h, k.dma_sems[9], v)
            st.wait("sync", o)
            st.run()
        aggregate_rows(k, c, ed, "gcn_sum", table, acc, F)
        st = k.stage("gcn_out")
        acc3 = blocks3(acc, ROW)
        v = st.v(lambda e: e.tensor_tensor(blocks3(h), blocks3(h), acc3[:, :, 0:F], ALU.add))
        v = st.v(lambda e: e.tensor_tensor(blocks3(h), blocks3(h), over(dinv[:, 0:NB], F), ALU.mult), v)
        v = st.v(lambda e: e.tensor_tensor(blocks3(h), blocks3(h), bias[:, :].unsqueeze(1).to_broadcast([P, NB, F]),
                                           ALU.add), v)
        v = st.v(lambda e: e.scalar_tensor_tensor(out=h[:, :], in0=h[:, :], scalar=0.0, in1=x[:, :], op0=ALU.max,
                                                  op1=ALU.add), v)
        v = layernorm_rows(k, st, own, "ln3", h, x, [v])
        full = (NB - 1) * P
        st.dma("sync", lambda e: e.dma_start(out[0:full, :].rearrange("(b p) f -> p b f", p=P),
                                             x[:, 0:full].rearrange("p (b f) -> p b f", f=F)), k.dma_sems[10], v)
        o = st.dma("sync", lambda e: e.dma_start(out[full:N, :], x[0:LAST, full:NP]), k.dma_sems[10], v)
        st.wait("sync", o)
        st.run()


def build(nc, w, out, tables):
    with ExitStack() as ctx:
        k = Kernel(nc, ctx)
        c = make_constants(k)
        ed = {"degree": k.sb("degree", NB)}
        x, acc = k.sb("x_rows", NP), k.sb("acc", NB * ROW)
        plan_tiles(k, c, w["dst"], w["recs"], ed)

        st = k.stage("load_x")
        full = (NB - 1) * P
        z = st.v(lambda e: e.memset(x[:, full:NP], 0.0))
        st.dma("sync", lambda e: e.dma_start(x[:, 0:full].rearrange("p (b f) -> p b f", f=F),
                                             w["x"][0:full, :].rearrange("(b p) f -> p b f", p=P)), k.dma_sems[8])
        o = st.dma("sync", lambda e: e.dma_start(x[0:LAST, full:NP], w["x"][full:N, :]), k.dma_sems[8], z)
        st.wait("sync", o)
        st.run()

        gin_layer(k, c, ed, w, x, acc, ed["degree"])

        with ExitStack() as own:
            h = k.sb("gat_h", NP, ctx=own)
            with ExitStack() as pre:
                st = k.stage("gat_in")
                cols, wt = k.sb("gat_in_cols", NP, ctx=pre), k.sb("gat_in_w", F, ctx=pre)
                bn = k.sb("gat_in_b", F, ctx=pre)
                st.dma("sync", lambda e: e.dma_start(bn[:, :], broadcast_row(w["L1_gnn_b_node"])), k.dma_sems[8])
                got = st.dma("sync", lambda e: e.dma_start(wt[:, :], w["L1_gnn_W_node"]), k.dma_sems[8])
                ready = rows_to_cols(k, st, c, x, cols, [])
                linear_rows(k, st, cols, wt[:, :], bn[:, :], h, [ready, got])
                st.run()
            gat_layer(k, c, ed, w, 0, h, acc, tables["gat"], tables["spill"],
                      lambda st, o, g, after: after)

            def residual(st, o, g, after):
                v = st.v(lambda e: e.tensor_tensor(g[:, :], g[:, :], x[:, :], ALU.add), after)
                layernorm_rows(k, st, o, "ln1", g, x, [v])
            gat_layer(k, c, ed, w, 1, h, acc, tables["gat"], tables["spill"], residual)

        relational_layer(k, c, ed, w, x, acc, (tables["left"], tables["right"], (w["attr"], w["types"])))
        gcn_layer(k, c, ed, w, x, acc, tables["gcn"], out)


WEIGHTS = ['L0_gnn_eps', 'L0_gnn_W1', 'L0_gnn_b1', 'L0_gnn_gamma1', 'L0_gnn_beta1', 'L0_gnn_a1', 'L0_gnn_W2',
           'L0_gnn_b2', 'L0_gnn_gamma2', 'L0_gnn_beta2', 'L0_gnn_a2', 'L1_gnn_W_node', 'L1_gnn_b_node',
           'L1_gnn_lyr_W', 'L1_gnn_att_src', 'L1_gnn_att_dst', 'L1_gnn_lyr_bias', 'L2_gnn_rel_emb', 'L2_gnn_W_l',
           'L2_gnn_b_l', 'L2_gnn_W_r', 'L2_gnn_b_r', 'L2_gnn_W_e', 'L2_gnn_att', 'L2_gnn_bias', 'L2_gnn_gate',
           'L2_gnn_g1', 'L2_gnn_bt1', 'L2_gnn_g2', 'L2_gnn_bt2', 'L2_gnn_Wf1', 'L2_gnn_bf1', 'L2_gnn_Wf2',
           'L2_gnn_bf2', 'L3_gnn_W', 'L3_gnn_b']


def kernel(**inputs):
    import concourse.bacc as bacc
    from concourse.bass_utils import run_bass_kernel_spmd

    def padded(a, value):
        return np.concatenate([a, np.full((EP - E,), value, a.dtype)])

    src, dst, typ = padded(inputs["src"], 0), padded(inputs["dst"], FAR), padded(inputs["edge_type_4"], 0)
    attr = np.concatenate([inputs["edge_attr_16"].T, np.zeros((DE, EP - E), np.float32)], axis=1)
    arrays = {"x": inputs["x"], "dst": dst, "recs": np.stack([src, dst, typ], axis=1), "types": typ,
              "attr": np.concatenate([attr] * R, axis=0)}
    for n in WEIGHTS:
        a = np.asarray(inputs[n])
        arrays[n] = a.reshape(1) if a.ndim == 0 else a
    nc = bacc.Bacc("TRN2", target_bir_lowering=False, num_devices=1)
    w, feed = {}, {}
    for n, a in arrays.items():
        a = np.ascontiguousarray(a)
        feed["in_" + n] = a
        w[n] = nc.dram_tensor("in_" + n, a.shape, mybir.dt.from_np(a.dtype), kind="ExternalInput").ap()
    out = nc.dram_tensor("out", (N, F), F32, kind="ExternalOutput").ap()
    tables = {
        "gat": nc.dram_tensor("gat_table", (NP, ROW), F32, kind="Internal").ap(),
        "gcn": nc.dram_tensor("gcn_table", (NP, F), F32, kind="Internal").ap(),
        "left": nc.dram_tensor("left_table", (NP * R, HC), F32, kind="Internal").ap(),
        "right": nc.dram_tensor("right_table", (NP * R, HC), F32, kind="Internal").ap(),
        "spill": nc.dram_tensor("spill", (P, TILES * ROW), F32, kind="Internal").ap(),
    }
    build(nc, w, out, tables)
    return run_bass_kernel_spmd(nc, [feed], core_ids=[0]).results[0]["out"]
```

```python
from contextlib import ExitStack

import numpy as np

import concourse.bass as bass
import concourse.mybir as mybir

F32 = mybir.dt.float32
I32 = mybir.dt.int32
BF16 = mybir.dt.bfloat16
ALU = mybir.AluOpType
ACT = mybir.ActivationFunctionType
AX_X = mybir.AxisListType.X
ENG = mybir.EngineType

P = 128
N, E, F = 6250, 100000, 128
NB = -(-N // P)
NP = NB * P
LAST = N - (NB - 1) * P
BATCH = 8
TILES = -(-((E + NB * (P - 1)) // P) // BATCH) * BATCH
G = -(-TILES // P)
SLOTS = G * P
IT = P * G
EP = -(-(E + P) // P) * P
EC = EP // P
CH = 448
R, H, HC, DE, DR = 4, 4, 512, 16, 8
TROW = F + 2
ROW = F + 1
LROW = HC + H
LAG = 3
BIG = 1e38
FAR = 1 << 20
LN_EPS = 1e-5

REG_WHY = "made on chip from counts whose range the shapes fix"


class Sem:

    def __init__(self, handle):
        self.handle, self.count = handle, 0


class Stage:

    ENGINES = ("sync", "scalar", "gpsimd", "tensor", "vector")

    def __init__(self, nc, ctx, name):
        self.nc, self.ctx, self.name = nc, ctx, name
        self.queue = {e: [] for e in self.ENGINES}
        self.done = {}

    def do(self, engine, emit, after=(), own=None):
        if engine not in self.done:
            self.done[engine] = Sem(self.ctx.enter_context(self.nc.semaphore(f"{self.name}_{engine}")))
        sem = self.done[engine]
        sem.count += 1
        self.queue[engine].append((emit, list(flat(after)), sem, 1, own))
        return (sem, sem.count)

    def v(self, emit, *after, own=None):
        return self.do("vector", emit, after, own)

    def s(self, emit, *after):
        return self.do("scalar", emit, after)

    def t(self, emit, *after):
        return self.do("tensor", emit, after)

    def g(self, emit, *after):
        return self.do("gpsimd", emit, after)

    def dma(self, engine, emit, sem, *after):
        sem.count += 16
        self.queue[engine].append((emit, list(flat(after)), sem, 16, None))
        return (sem, sem.count)

    def plain(self, engine, emit, *after):
        self.queue[engine].append((emit, list(flat(after)), None, 0, None))

    def wait(self, engine, *after):
        self.queue[engine].append((None, list(flat(after)), None, 0, None))

    def run(self):
        def play(name):
            def body(eng):
                seen = {}
                for emit, after, sem, inc, own in self.queue[name]:
                    for ticket in after:
                        if seen.get(ticket[0], 0) < ticket[1]:
                            eng.wait_ge(ticket[0].handle, ticket[1])
                            seen[ticket[0]] = ticket[1]
                    if emit is not None:
                        made = emit(eng)
                        if own is not None:
                            made.wait_op(own[0].handle, own[1], "sem-ge")
                            seen[own[0]] = max(seen.get(own[0], 0), own[1])
                        if sem is not None:
                            made.then_inc(sem.handle, inc)
            return body

        with self.nc.Block() as block:
            for name in self.ENGINES:
                if self.queue[name]:
                    getter = {"sync": block.sync, "scalar": block.scalar, "gpsimd": block.gpsimd,
                              "tensor": block.tensor, "vector": block.vector}[name]
                    getter(play(name))


def flat(tickets):
    for x in tickets:
        if x is None:
            continue
        if isinstance(x, tuple) and len(x) == 2 and isinstance(x[0], Sem):
            yield x
        else:
            yield from flat(x)


class Ring:

    def __init__(self, items):
        self.items, self.free, self.n = items, [None] * len(items), -1

    def take(self):
        self.n += 1
        k = self.n % len(self.items)
        return k, self.items[k], self.free[k]


class Kernel:
    def __init__(self, nc, ctx):
        self.nc, self.ctx, self.named = nc, ctx, {}
        self.psum = [ctx.enter_context(nc.psum_tensor(f"bank{k}", [P, 512], F32)) for k in range(8)]
        self.dma_sems = [Sem(ctx.enter_context(nc.semaphore(f"dma{k}"))) for k in range(16)]
        self.pool_sems = [Sem(ctx.enter_context(nc.semaphore(f"pool_dma{k}"))) for k in range(12)]

    def stage(self, name):
        return Stage(self.nc, self.ctx, name)

    def sb(self, name, cols, dt=F32, rows=P, ctx=None):
        self.named[name] = self.named.get(name, 0) + 1
        if self.named[name] > 1:
            name = f"{name}_{self.named[name]}"
        return (ctx or self.ctx).enter_context(self.nc.sbuf_tensor(name, [rows, cols], dt))

    def regs(self, engine, row, first, count, top):
        return self.nc.values_load_multi_w_load_instructions(
            row[0:1, first:first + count], engines=[engine], min_val=0, max_val=top,
            skip_runtime_bounds_check_because=REG_WHY)[1]


def blocks3(t, w=F):
    return t[:, :].rearrange("p (b f) -> p b f", f=w)


def split_bf16(st, x, rest, part, after):
    v = st.v(lambda e: e.tensor_copy(part(0), x), after)
    v = st.v(lambda e: e.tensor_tensor(rest, x, part(0), ALU.subtract), v)
    v = st.v(lambda e: e.tensor_copy(part(1), rest), v)
    v = st.v(lambda e: e.tensor_tensor(rest, rest, part(1), ALU.subtract), v)
    return st.v(lambda e: e.tensor_copy(part(2), rest), v)


def repeat_rows(rows):
    return rows.unsqueeze(1).to_broadcast([rows.shape[0], R, rows.shape[1]])


def over(col, w):
    return col.unsqueeze(2).to_broadcast([col.shape[0], col.shape[1], w])


def make_constants(k):
    c = {}
    for name in ("ident", "before", "shift_up", "shift_down", "ones"):
        c[name] = k.sb(name, P)
    c["node_iota"] = k.sb("node_iota", P)
    c["slot_col"] = k.sb("slot_col", 1)
    st = k.stage("constants")
    tmp = k.sb("iota_int", P + 1, I32)
    zero = [st.g(lambda e, t=c[n]: e.memset(t[:, :], 0.0)) for n in ("ident", "shift_up", "shift_down")]
    one = [st.g(lambda e, t=c[n]: e.memset(t[:, :], 1.0)) for n in ("ones", "before")]

    def select(t, op, base, step, chan, fill, after):
        return st.g(lambda e: e.affine_select(out=t[:, :], in_=t[:, :], pattern=[[step, P]], compare_op=op,
                                              fill=fill, base=base, channel_multiplier=chan), after)
    select(c["ident"], ALU.not_equal, 0, 1, -1, 1.0, zero)
    select(c["shift_up"], ALU.not_equal, -1, 1, -1, 1.0, zero)
    select(c["shift_down"], ALU.not_equal, 1, 1, -1, 1.0, zero)
    select(c["before"], ALU.is_gt, 0, 1, -1, 0.0, one)
    a = st.g(lambda e: e.iota(tmp[:, 0:P], pattern=[[1, P]], base=0, channel_multiplier=0))
    b = st.g(lambda e: e.iota(tmp[:, P:P + 1], pattern=[[0, 1]], base=0, channel_multiplier=1))
    st.v(lambda e: e.tensor_copy(c["node_iota"][:, :], tmp[:, 0:P]), a)
    st.v(lambda e: e.tensor_copy(c["slot_col"][:, :], tmp[:, P:P + 1]), b)
    st.run()
    return c


def to_slots(k, st, c, out, src, after, banks=(0, 1)):
    view = out[:, :].rearrange("q (p g) -> q g p", g=G)
    done = []
    for bank, lo, hi in ((banks[0], 0, 4), (banks[1], 4, G)):
        ps = k.psum[bank]
        for g in range(lo, hi):
            t = st.t(lambda e, g=g, lo=lo, ps=ps: e.transpose(ps[:, (g - lo) * P:(g - lo + 1) * P], src(g),
                                                              c["ident"][:, :]), after)
        done.append(st.v(lambda e, lo=lo, hi=hi, ps=ps: e.tensor_copy(
            view[:, lo:hi, :], ps[:, 0:(hi - lo) * P].rearrange("q (g p) -> q g p", p=P)), t))
    return done


def to_scan(k, st, c, out, src, after, banks=(0, 1)):
    view = src.rearrange("q (p g) -> q g p", g=G)
    done = []
    for bank, lo, hi in ((banks[0], 0, 4), (banks[1], 4, G)):
        ps = k.psum[bank]
        for g in range(lo, hi):
            t = st.t(lambda e, g=g, lo=lo, ps=ps: e.transpose(ps[:, (g - lo) * P:(g - lo + 1) * P], view[:, g, :],
                                                              c["ident"][:, :]), after)
        done.append(st.v(lambda e, lo=lo, hi=hi, ps=ps: e.tensor_copy(
            out[:, lo * P:hi * P], ps[:, 0:(hi - lo) * P]), t))
    return done


def plan_tiles(k, c, dst_all, recs, ed):
    for n in ("acc_row", "blk_row", "edge_row"):
        ed[n] = k.sb(n, IT, I32, rows=1)
    ed["src"] = k.sb("src_idx", IT, I32)
    for n in ("local", "valid", "type", "dst"):
        ed[n] = k.sb("e_" + n, IT)
    for n in ("same_prev", "same_next", "type_scan", "add_prev", "add_next", "pre_mul", "suf_mul", "pre_add",
              "suf_add"):
        ed[n] = k.sb(n, SLOTS)
    ed["flags"] = k.sb("flag_rows", 4 * P, rows=R)
    with ExitStack() as own:
        sb = lambda n, w, dt=F32, rows=P: k.sb(n, w, dt, rows, own)
        st = k.stage("count")
        dst_i, dst_f, junk = sb("dst_i", EC, I32), sb("dst_f", EC), sb("junk", EC)
        cnt = sb("cnt", NB + 1)
        got = st.dma("sync", lambda e: e.dma_start(dst_i[:, :], dst_all.rearrange("(p j) -> p j", j=EC)), k.dma_sems[0])
        cast = st.v(lambda e: e.tensor_copy(dst_f[:, :], dst_i[:, :]), got)
        t = st.v(lambda e: e.memset(cnt[:, 0:1], 0.0))
        for b in range(1, NB + 1):
            t = st.v(lambda e, b=b: e.tensor_scalar(junk[:, :], dst_f[:, :], float(P * b), 0.0, ALU.is_lt, ALU.add,
                                                    accum_out=cnt[:, b:b + 1]), cast, t)
        ps = k.psum[0]
        st.t(lambda e: e.matmul(ps[0:NB, 0:1], cnt[:, 0:NB], c["ones"][:, 0:1], start=True, stop=True), t)
        m = st.t(lambda e: e.matmul(ps[0:NB, 1:2], cnt[:, 1:NB + 1], c["ones"][:, 0:1], start=True, stop=True))
        col = sb("block_cols", 8)
        coli = sb("block_cols_int", 2, I32)
        B = slice(0, NB)
        v = st.v(lambda e: e.tensor_copy(col[B, 0:2], ps[B, 0:2]), m)
        v = n_edges = st.v(lambda e: e.tensor_tensor(col[B, 2:3], col[B, 1:2], col[B, 0:1], ALU.subtract), v)
        v = st.v(lambda e: e.tensor_scalar(coli[B, 0:1], col[B, 2:3], float(P - 1), None, ALU.add), v)
        v = st.v(lambda e: e.tensor_scalar(coli[B, 1:2], coli[B, 0:1], 7, None, ALU.arith_shift_right), v)
        v = tiles = st.v(lambda e: e.tensor_copy(col[B, 3:4], coli[B, 1:2]), v)
        v = st.v(lambda e: e.scalar_tensor_tensor(out=col[B, 4:5], in0=col[B, 3:4], scalar=-float(P), in1=col[B, 2:3],
                                                  op0=ALU.mult, op1=ALU.add), v)
        st.t(lambda e: e.matmul(ps[0:NB, 2:3], c["before"][B, B], col[B, 3:4], start=True, stop=True), v)
        m = st.t(lambda e: e.matmul(ps[0:NB, 3:4], c["shift_up"][B, B], col[B, 4:5], start=True, stop=True))
        v = st.v(lambda e: e.tensor_copy(col[B, 5:7], ps[B, 2:4]), m)
        tile_i, tile_f = sb("tile_i", IT, I32), sb("tile_f", IT)
        ti = st.g(lambda e: e.iota(tile_i[:, :], pattern=[[1, IT]], base=0, channel_multiplier=0))
        tf = st.v(lambda e: e.tensor_copy(tile_f[:, :], tile_i[:, :]), ti)
        passed = sb("passed", IT)
        pas = st.v(lambda e: e.tensor_scalar(passed[B, :], tile_f[B, :], col[B, 5:6], None, ALU.is_ge), v, tf)
        w_jump, w_n = sb("w_jump", P), sb("w_n", P)
        w1 = st.v(lambda e: e.tensor_scalar(w_jump[B, :], c["ones"][B, :], col[B, 6:7], None, ALU.mult), v)
        w2 = st.v(lambda e: e.tensor_scalar(w_n[B, :], c["ones"][B, :], col[B, 2:3], None, ALU.mult), n_edges)
        half = IT // 2
        for j, w in enumerate((c["ones"], w_jump, w_n)):
            for h in range(2):
                m = st.t(lambda e, j=j, h=h, w=w: e.matmul(k.psum[1 + 2 * j + h][:, 0:half], w[B, :],
                                                           passed[B, h * half:(h + 1) * half], start=True, stop=True),
                         pas, w1, w2)
        blk, first, left, tmp = sb("t_blk", IT), sb("t_first", IT), sb("t_left", IT), sb("t_tmp", IT)
        outs = []
        for h in range(2):
            s = slice(h * half, (h + 1) * half)
            a = st.v(lambda e, s=s, h=h: e.tensor_scalar(blk[:, s], k.psum[1 + h][:, 0:half], -1.0, None, ALU.add), m)
            b_ = st.v(lambda e, s=s, h=h: e.scalar_tensor_tensor(
                out=first[:, s], in0=tile_f[:, s], scalar=float(P), in1=k.psum[3 + h][:, 0:half], op0=ALU.mult,
                op1=ALU.add), m, tf)
            b_ = st.v(lambda e, s=s: e.tensor_scalar(first[:, s], first[:, s], float(E), None, ALU.min), b_)
            b_ = st.v(lambda e, s=s, h=h: e.tensor_tensor(left[:, s], k.psum[5 + h][:, 0:half], first[:, s],
                                                          ALU.subtract), b_)
            outs += [a, b_]
        va = st.v(lambda e: e.tensor_scalar(ed["valid"][:, :], left[:, :], c["slot_col"][:, 0:1], None, ALU.is_gt), outs)
        st.v(lambda e: e.tensor_scalar(ed["acc_row"][:, :], blk[0:1, :], float(ROW), None, ALU.mult), outs)
        st.v(lambda e: e.tensor_scalar(ed["blk_row"][:, :], blk[0:1, :], float(P), None, ALU.mult), outs)
        st.v(lambda e: e.tensor_copy(ed["edge_row"][:, :], first[0:1, :]), outs)
        st.run()

        st = k.stage("records")
        rec_i, rec_f = sb("rec_i", G * P * 3, I32), sb("rec_f", G * P * 3)
        starts, by_part = sb("starts", G, I32), first[:, :].rearrange("q (p g) -> q g p", g=G)
        for g in range(G):
            m = st.t(lambda e, g=g: e.matmul(k.psum[7][:, g:g + 1], by_part[0:1, g, :], c["ones"][0:1, 0:1],
                                             start=True, stop=True))
        at_g = st.v(lambda e: e.tensor_scalar(starts[:, :], k.psum[7][:, 0:G], 3.0, None, ALU.mult), m)
        for g in range(G):
            got = st.dma("gpsimd", lambda e, g=g: e.indirect_dma_start(
                rec_i[:, g * 3 * P:(g + 1) * 3 * P], None, recs[:, :].rearrange("(a b) c -> a (b c)", b=P),
                bass.IndirectOffsetOnAxis(ap=starts[:, g:g + 1], axis=1)), k.pool_sems[0], at_g)
        cast = st.v(lambda e: e.tensor_copy(rec_f[:, :], rec_i[:, :]), got)
        recv = rec_f[:, :].rearrange("p (g q c) -> p g q c", g=G, c=3)
        st.v(lambda e: e.tensor_copy(ed["type_scan"][:, :].rearrange("p (g q) -> p g q", g=G), recv[:, :, :, 2]), cast)
        srcf, key = sb("src_f", IT), sb("key", IT)
        a = to_slots(k, st, c, srcf, lambda g: recv[:, g, :, 0], [cast], (0, 1))
        b_ = to_slots(k, st, c, ed["dst"], lambda g: recv[:, g, :, 1], [cast], (2, 3))
        t_ = to_slots(k, st, c, ed["type"], lambda g: recv[:, g, :, 2], [cast], (4, 5))
        st.v(lambda e: e.tensor_tensor(ed["src"][:, :], srcf[:, :], ed["valid"][:, :], ALU.mult), a)
        x = st.v(lambda e: e.scalar_tensor_tensor(out=ed["dst"][:, :], in0=ed["dst"][:, :], scalar=1.0,
                                                  in1=ed["valid"][:, :], op0=ALU.add, op1=ALU.mult), b_)
        y = st.v(lambda e: e.tensor_tensor(tmp[:, :], blk[:, :], ed["valid"][:, :], ALU.mult))
        ky = st.v(lambda e: e.tensor_scalar(key[:, :], ed["dst"][:, :], -1.0, None, ALU.add), x)
        y = st.v(lambda e: e.scalar_tensor_tensor(out=ed["local"][:, :], in0=tmp[:, :], scalar=-float(P),
                                                  in1=key[:, :], op0=ALU.mult, op1=ALU.add), y, ky)
        st.v(lambda e: e.tensor_scalar(ed["dst"][:, :], key[:, :], 0.0, None, ALU.max), ky)
        kx = sb("key_scan", SLOTS + 2)
        kk = to_scan(k, st, c, kx[:, 1:SLOTS + 1], key[:, :], [ky], (6, 7))
        st.t(lambda e: e.matmul(k.psum[0][:, 0:1], c["shift_up"][:, :], kx[:, SLOTS:SLOTS + 1], start=True, stop=True), kk, a)
        m = st.t(lambda e: e.matmul(k.psum[0][:, 1:2], c["shift_down"][:, :], kx[:, 1:2], start=True, stop=True))
        st.v(lambda e: e.tensor_copy(kx[:, 0:1], k.psum[0][:, 0:1]), m)
        v = st.v(lambda e: e.tensor_copy(kx[:, SLOTS + 1:SLOTS + 2], k.psum[0][:, 1:2]), m)
        for same, add, mul, full, lo, back in (("same_prev", "add_prev", "pre_mul", "pre_add", 0, False),
                                               ("same_next", "add_next", "suf_mul", "suf_add", 2, True)):
            d = slice(None, None, -1) if back else slice(None)
            q = st.v(lambda e, same=same, lo=lo: e.tensor_tensor(ed[same][:, :], kx[:, 1:SLOTS + 1],
                                                                 kx[:, lo:lo + SLOTS], ALU.is_equal), v, kk)
            st.v(lambda e, same=same, add=add: e.tensor_scalar(ed[add][:, :], ed[same][:, :], -1.0, BIG, ALU.add,
                                                               ALU.mult), q)
            q = st.v(lambda e, same=same, mul=mul, d=d: e.tensor_tensor_scan(
                ed[mul][:, d], ed[same][:, d], ed[same][:, d], 1.0, ALU.mult, ALU.min), q)
            st.v(lambda e, mul=mul, full=full: e.tensor_scalar(ed[full][:, :], ed[mul][:, :], -1.0, BIG, ALU.add,
                                                               ALU.mult), q)
        spread = sb("flag_cols", 4 * R)
        zs = []
        for j, (n, cix) in enumerate((("pre_add", SLOTS - 1), ("suf_add", 0), ("pre_mul", SLOTS - 1), ("suf_mul", 0))):
            zs.append(st.v(lambda e, j=j, n=n, cix=cix: e.tensor_copy(
                spread[:, j * R:(j + 1) * R], ed[n][:, cix:cix + 1].to_broadcast([P, R])), (st.done["vector"], st.done["vector"].count)))
        for j in range(4):
            m = st.t(lambda e, j=j: e.transpose(k.psum[1][0:R, j * P:(j + 1) * P], spread[:, j * R:(j + 1) * R],
                                                c["ident"][:, :]), zs)
        st.v(lambda e: e.tensor_copy(ed["flags"][:, :], k.psum[1][0:R, 0:4 * P]), m)
        st.run()


def segment_reduce(k, st, c, ed, own, tag, kind, vals, after):
    C = len(vals)
    big = kind == "max"
    step = (ed["add_prev"], ed["add_next"]) if big else (ed["same_prev"], ed["same_next"])
    reach = (ed["pre_add"], ed["suf_add"]) if big else (ed["pre_mul"], ed["suf_mul"])
    op0, op1 = (ALU.add, ALU.max) if big else (ALU.mult, ALU.add)
    neutral = -BIG if big else 0.0
    outs = [[k.sb(f"{tag}_{d}{j}", SLOTS, ctx=own) for j in range(C)] for d in "fb"]
    ends = k.sb(f"{tag}_ends", 2 * C, ctx=own)
    rows = k.sb(f"{tag}_rows", 2 * P, rows=C, ctx=own)
    carry_rows = k.sb(f"{tag}_carry_rows", 2 * P + 2, rows=C, ctx=own)
    carry = k.sb(f"{tag}_carry", 2 * C, ctx=own)
    t = []
    for w in (0, 1):
        d = slice(None, None, -1) if w else slice(None)
        for j in range(C):
            q = st.v(lambda e, w=w, j=j, d=d: e.tensor_tensor_scan(outs[w][j][:, d], step[w][:, d], vals[j][:, d],
                                                                   neutral, op0, op1), after)
            cix = 0 if w else SLOTS - 1
            t.append(st.v(lambda e, w=w, j=j, cix=cix: e.tensor_copy(ends[:, w * C + j:w * C + j + 1],
                                                                     outs[w][j][:, cix:cix + 1]), q))
    ps = k.psum[0]
    for w in (0, 1):
        m = st.t(lambda e, w=w: e.transpose(ps[0:C, w * P:(w + 1) * P], ends[:, w * C:(w + 1) * C],
                                            c["ident"][:, :]), t)
    z = [st.v(lambda e: e.memset(carry_rows[:, 0:1], neutral)),
         st.v(lambda e: e.memset(carry_rows[:, 2 * P + 1:2 * P + 2], neutral)),
         st.v(lambda e: e.tensor_copy(rows[:, :], ps[0:C, 0:2 * P]), m)]
    f0 = 0 if big else 2
    z.append(st.v(lambda e: e.tensor_tensor_scan(carry_rows[:, 1:P + 1], ed["flags"][0:C, f0 * P:(f0 + 1) * P],
                                                 rows[:, 0:P], neutral, op0, op1), z))
    z.append(st.v(lambda e: e.tensor_tensor_scan(carry_rows[:, P + 1:2 * P + 1][:, ::-1],
                                                 ed["flags"][0:C, (f0 + 1) * P:(f0 + 2) * P][:, ::-1],
                                                 rows[:, P:2 * P][:, ::-1], neutral, op0, op1), z))
    st.t(lambda e: e.transpose(k.psum[1][:, 0:C], carry_rows[:, 0:P], c["ident"][0:C, 0:C]), z)
    m = st.t(lambda e: e.transpose(k.psum[1][:, C:2 * C], carry_rows[:, P + 2:2 * P + 2], c["ident"][0:C, 0:C]), z)
    cc = st.v(lambda e: e.tensor_copy(carry[:, :], k.psum[1][:, 0:2 * C]), m)
    done = []
    for j in range(C):
        both = []
        for w in (0, 1):
            both.append(st.v(lambda e, w=w, j=j: e.scalar_tensor_tensor(
                out=outs[w][j][:, :], in0=reach[w][:, :], scalar=carry[:, w * C + j:w * C + j + 1],
                in1=outs[w][j][:, :], op0=op0, op1=op1), cc))
        if not big:
            both.append(st.v(lambda e, j=j: e.tensor_tensor(outs[1][j][:, :], outs[1][j][:, :], vals[j][:, :],
                                                            ALU.subtract), both))
        done.append(st.v(lambda e, j=j: e.tensor_tensor(outs[0][j][:, :], outs[0][j][:, :], outs[1][j][:, :],
                                                        ALU.max if big else ALU.add), both))
    return outs[0], done


def rows_to_cols(k, st, c, rows, cols, after):
    ring = Ring([6, 7])
    done = []
    for lo in range(0, NB, 4):
        hi = min(lo + 4, NB)
        s, bank, free = ring.take()
        for b in range(lo, hi):
            t = st.t(lambda e, b=b, lo=lo, bank=bank: e.transpose(
                k.psum[bank][:, (b - lo) * P:(b - lo + 1) * P], rows[:, b * P:(b + 1) * P], c["ident"][:, :]),
                after, free)
        if (lo // 4) % 2:
            d = st.s(lambda e, lo=lo, hi=hi, bank=bank: e.copy(cols[:, lo * P:hi * P], k.psum[bank][:, 0:(hi - lo) * P]), t)
        else:
            d = st.v(lambda e, lo=lo, hi=hi, bank=bank: e.tensor_copy(cols[:, lo * P:hi * P],
                                                                      k.psum[bank][:, 0:(hi - lo) * P]), t)
        ring.free[s] = d
        done.append(d)
    return done


def linear_rows(k, st, cols, weight, bias_row, out, after):
    ring = Ring([4, 5])
    done = []
    for lo in range(0, NB, 4):
        hi = min(lo + 4, NB)
        s, bank, free = ring.take()
        for b in range(lo, hi):
            t = st.t(lambda e, b=b, lo=lo, bank=bank: e.matmul(
                k.psum[bank][:, (b - lo) * P:(b - lo + 1) * P], cols[:, b * P:(b + 1) * P], weight,
                start=True, stop=True), after, free)
        view = lambda x, lo=lo, hi=hi: x[:, lo * P:hi * P].rearrange("p (b f) -> p b f", f=F)
        if bias_row is None:
            d = st.s(lambda e, lo=lo, hi=hi, bank=bank: e.copy(out[:, lo * P:hi * P],
                                                               k.psum[bank][:, 0:(hi - lo) * P]), t)
        else:
            d = st.v(lambda e, lo=lo, hi=hi, bank=bank, view=view: e.tensor_tensor(
                view(out), k.psum[bank][:, 0:(hi - lo) * P].rearrange("p (b f) -> p b f", f=F),
                bias_row.unsqueeze(1).to_broadcast([P, hi - lo, F]), ALU.add), t, after)
        ring.free[s] = d
        done.append(d)
    return done


def layernorm_rows(k, st, own, tag, x, out, after, gain=None, shift=None):
    x3, o3 = blocks3(x), blocks3(out)
    s = k.sb(tag + "_stat", 3 * NB, ctx=own)
    v = st.v(lambda e: e.tensor_reduce(s[:, 0:NB], x3, AX_X, ALU.add), after)
    v = st.v(lambda e: e.tensor_scalar(s[:, 0:NB], s[:, 0:NB], 1.0 / F, None, ALU.mult), v)
    bounds = [NB * j // 4 for j in range(5)]
    parts = list(zip(bounds, bounds[1:]))
    mean = v
    cent = [st.v(lambda e, lo=lo, hi=hi: e.tensor_tensor(x3[:, lo:hi, :], x3[:, lo:hi, :], over(s[:, lo:hi], F),
                                                         ALU.subtract), mean) for lo, hi in parts]
    squared = [st.s(lambda e, lo=lo, hi=hi: e.square(o3[:, lo:hi, :], x3[:, lo:hi, :]), t, after)
               for (lo, hi), t in zip(parts, cent)]
    v = [st.v(lambda e, lo=lo, hi=hi: e.tensor_reduce(s[:, NB + lo:NB + hi], o3[:, lo:hi, :], AX_X, ALU.add), t)
         for (lo, hi), t in zip(parts, squared)]
    v = st.v(lambda e: e.tensor_scalar(s[:, NB:2 * NB], s[:, NB:2 * NB], 1.0 / F, LN_EPS, ALU.mult, ALU.add), v)
    v = st.s(lambda e: e.sqrt(s[:, 2 * NB:3 * NB], s[:, NB:2 * NB]), v)
    v = st.v(lambda e: e.reciprocal(s[:, 2 * NB:3 * NB], s[:, 2 * NB:3 * NB]), v)
    v = st.v(lambda e: e.tensor_tensor(o3, x3, over(s[:, 2 * NB:3 * NB], F), ALU.mult), v)
    if gain is not None:
        v = st.v(lambda e: e.tensor_tensor(o3, o3, gain.unsqueeze(1).to_broadcast([P, NB, F]), ALU.mult), v)
        v = st.v(lambda e: e.tensor_tensor(o3, o3, shift.unsqueeze(1).to_broadcast([P, NB, F]), ALU.add), v)
    return v


def store_rows(k, st, engine, table, rows, sem, after, width=F):
    return st.dma(engine, lambda e: e.dma_start(table[:, :].rearrange("(b p) f -> p b f", p=P),
                                                rows[:, :].rearrange("p (b f) -> p b f", f=width)), sem, after)


def broadcast_row(vec):
    return vec.partition_broadcast(P)


def aggregate_rows(k, c, ed, name, table, acc, width):
    with ExitStack() as own:
        st = k.stage(name)
        NG, NS = 8, 6
        gathered = Ring([k.sb(f"{name}_rows{j}", width, ctx=own) for j in range(NG)])
        hot = Ring([k.sb(f"{name}_hot{j}", P, ctx=own) for j in range(NS)])
        bank = Ring([0, 1, 2, 3, 4, 5])
        zero = st.v(lambda e: e.memset(acc[:, :], 0.0))
        ones = [st.v(lambda e, j=j: e.memset(gathered.items[j][:, F:width], 1.0)) for j in range(NG)] if width > F else []
        last_add, hold, pend = zero, [], []

        def add_up(item):
            i, bk, slot, product = item
            nonlocal last_add
            if i % BATCH == 0:
                st.plain("vector", lambda e: (hold.clear(), hold.extend(k.regs(ENG.DVE, ed["acc_row"], i, BATCH,
                                                                               (NB - 1) * ROW))))
            last_add = st.v(lambda e: e.tensor_tensor(acc[:, bass.ds(hold[i % BATCH], width)],
                                                      acc[:, bass.ds(hold[i % BATCH], width)],
                                                      k.psum[bk][:, 0:width], ALU.add), product, own=last_add)
            bank.free[slot] = last_add

        for i in range(TILES):
            gs, rows, gfree = gathered.take()
            got = st.dma("gpsimd", lambda e, rows=rows, i=i: e.indirect_dma_start(
                rows[:, 0:F], None, table[:, :], bass.IndirectOffsetOnAxis(ap=ed["src"][:, i:i + 1], axis=0)),
                k.pool_sems[gs], gfree)
            hs, s, hfree = hot.take()
            made = st.v(lambda e, s=s, i=i: e.tensor_scalar(s[:, :], c["node_iota"][:, :], ed["local"][:, i:i + 1],
                                                            None, ALU.is_equal), hfree)
            bs, bk, bfree = bank.take()
            prod = st.t(lambda e, s=s, rows=rows, bk=bk: e.matmul(k.psum[bk][:, 0:width], s[:, :], rows[:, 0:width],
                                                                  start=True, stop=True), got, made, bfree, ones)
            gathered.free[gs] = hot.free[hs] = prod
            pend.append((i, bk, bs, prod))
            if len(pend) > LAG:
                add_up(pend.pop(0))
        for item in pend:
            add_up(item)
        st.run()


def gin_layer(k, c, ed, w, x, acc, degree):
    aggregate_rows(k, c, ed, "gin_sum", w["x"], acc, F + 1)
    with ExitStack() as own:
        st = k.stage("gin_mlp")
        acc3 = blocks3(acc, ROW)
        par = k.sb("gin_par", 16, ctx=own)
        w1, w2 = k.sb("gin_w1", F, ctx=own), k.sb("gin_w2", F, ctx=own)
        loads = [(par[:, 0:1], broadcast_row(w["L0_gnn_eps"])), (par[:, 1:2], broadcast_row(w["L0_gnn_a1"])),
                 (par[:, 2:3], broadcast_row(w["L0_gnn_a2"])), (w1[:, :], w["L0_gnn_W1"]), (w2[:, :], w["L0_gnn_W2"])]
        for j, n in enumerate(("b1", "gamma1", "beta1", "b2", "gamma2", "beta2")):
            loads.append((par[:, 3 + j:4 + j], w["L0_gnn_" + n].unsqueeze(1)))
        for dst, src in loads:
            par_in = st.dma("sync", lambda e, dst=dst, src=src: e.dma_start(dst, src), k.dma_sems[8])
        st.v(lambda e: e.tensor_copy(degree[:, :], acc3[:, :, F:F + 1].rearrange("p b o -> p (b o)")))
        h, cols = k.sb("gin_h", NP, ctx=own), k.sb("gin_cols", NP, ctx=own)
        v = st.v(lambda e: e.tensor_scalar(par[:, 0:1], par[:, 0:1], 1.0, None, ALU.add), par_in)
        v = st.v(lambda e: e.scalar_tensor_tensor(out=blocks3(h), in0=blocks3(x), scalar=par[:, 0:1],
                                                  in1=acc3[:, :, 0:F], op0=ALU.mult, op1=ALU.add), v)
        ready = rows_to_cols(k, st, c, h, cols, [v])
        for layer, (wt, b0, slope) in enumerate(((w1, 3, 1), (w2, 6, 2))):
            ring, done = Ring([0, 1, 2, 3]), []
            for j in range(NP // CH):
                s, bk, free = ring.take()
                t = st.t(lambda e, j=j, bk=bk, wt=wt: e.matmul(k.psum[bk][:, 0:CH], wt[:, :],
                                                               cols[:, j * CH:(j + 1) * CH], start=True, stop=True),
                         ready, free, par_in)
                ring.free[s] = st.s(lambda e, j=j, bk=bk, b0=b0: e.activation(
                    h[:, j * CH:(j + 1) * CH], k.psum[bk][:, 0:CH], ACT.Identity, bias=par[:, b0:b0 + 1]), t)
                done.append(ring.free[s])
            q = lambda a: par[:, a:a + 1]
            v = st.v(lambda e: e.tensor_reduce(q(9), h[:, 0:N], AX_X, ALU.add), done)
            v = st.v(lambda e: e.tensor_scalar(q(9), q(9), 1.0 / N, None, ALU.mult), v)
            v = st.v(lambda e: e.tensor_scalar(h[:, :], h[:, :], q(9), None, ALU.subtract), v)
            v = st.s(lambda e: e.activation(cols[:, 0:N], h[:, 0:N], ACT.Square, accum_out=q(10)), v)
            v = st.v(lambda e: e.tensor_scalar(q(10), q(10), 1.0 / N, LN_EPS, ALU.mult, ALU.add), v)
            v = st.s(lambda e: e.sqrt(q(11), q(10)), v)
            v = st.v(lambda e: e.reciprocal(q(12), q(11)), v)
            v = st.v(lambda e, b0=b0: e.tensor_tensor(q(12), q(12), q(b0 + 1), ALU.mult), v)
            v = st.v(lambda e, b0=b0: e.tensor_scalar(h[:, :], h[:, :], q(12), q(b0 + 2), ALU.mult, ALU.add), v)
            v = st.v(lambda e, slope=slope: e.tensor_scalar(cols[:, :], h[:, :], 0.0, q(slope), ALU.min, ALU.mult), v)
            v = st.v(lambda e: e.scalar_tensor_tensor(out=cols[:, :], in0=h[:, :], scalar=0.0, in1=cols[:, :],
                                                      op0=ALU.max, op1=ALU.add), v)
            ready = [v]
        done = rows_to_cols(k, st, c, cols, h, ready)
        v = st.v(lambda e: e.tensor_tensor(h[:, :], h[:, :], x[:, :], ALU.add), done)
        layernorm_rows(k, st, own, "ln0", h, x, [v])
        st.run()


def gat_layer(k, c, ed, w, layer, h_in, acc, table, spill, combine):
    name = f"gat{layer}"
    with ExitStack() as own:
        g = h_in
        node = k.sb(name + "_node", 3 * NB, ctx=own)
        nd = lambda j: node[:, j * NB:(j + 1) * NB]
        sp, dp, sdp = (k.sb(f"{name}_{n}", IT, ctx=own) for n in ("src_term", "dst_term", "self_term"))
        bias = k.sb(name + "_bias", F, ctx=own)
        with ExitStack() as pre:
            st = k.stage(name + "_nodes")
            cols = k.sb(name + "_cols", NP, ctx=pre)
            wt = k.sb(name + "_w", F, ctx=pre)
            att = k.sb(name + "_att", 2 * F, ctx=pre)
            for dst, src in ((wt[:, :], w["L1_gnn_lyr_W"][layer]), (att[:, 0:F], broadcast_row(w["L1_gnn_att_src"][layer])),
                             (att[:, F:2 * F], broadcast_row(w["L1_gnn_att_dst"][layer])),
                             (bias[:, :], broadcast_row(w["L1_gnn_lyr_bias"][layer]))):
                got = st.dma("sync", lambda e, dst=dst, src=src: e.dma_start(dst, src), k.dma_sems[8])
            ready = rows_to_cols(k, st, c, h_in, cols, [])
            done = linear_rows(k, st, cols, wt[:, :], None, g, [ready, got])
            v = done
            for j in (0, 1):
                v = st.v(lambda e, j=j: e.tensor_tensor(blocks3(cols), blocks3(g), att[:, j * F:(j + 1) * F].unsqueeze(
                    1).to_broadcast([P, NB, F]), ALU.mult), v)
                v = st.v(lambda e, j=j: e.tensor_reduce(nd(j), blocks3(cols), AX_X, ALU.add), v)
            tail = k.sb(name + "_tail", 2 * NB, ctx=pre)
            t3 = tail[:, :].rearrange("p (b o) -> p b o", o=2)
            a = st.v(lambda e: e.memset(tail[:, :], 1.0))
            a = st.v(lambda e: e.tensor_copy(t3[:, :, 1], nd(0)), a, v)
            tv = table[:, :].rearrange("(b p) f -> p b f", p=P)
            o1 = st.dma("sync", lambda e: e.dma_start(tv[:, :, 0:F], blocks3(g)), k.dma_sems[9], done)
            o2 = st.dma("sync", lambda e: e.dma_start(tv[:, :, F:TROW], t3), k.dma_sems[9], a)
            st.wait("sync", o1, o2)
            st.run()

        with ExitStack() as mid:
            st = k.stage(name + "_gather")
            dB, sB = acc, k.sb(name + "_sB", NP, ctx=mid)
            ring, done = Ring([4, 5, 6, 7]), []
            for j, out in ((1, dB), (0, sB)):
                for lo in range(0, NB, 4):
                    hi = min(lo + 4, NB)
                    s, bk, free = ring.take()
                    for b in range(lo, hi):
                        t = st.t(lambda e, b=b, lo=lo, bk=bk, j=j: e.matmul(
                            k.psum[bk][:, (b - lo) * P:(b - lo + 1) * P], nd(j)[:, b:b + 1].to_broadcast([P, P]),
                            c["ident"][:, :], start=True, stop=True), free)
                    ring.free[s] = st.s(lambda e, lo=lo, hi=hi, bk=bk, out=out: e.copy(
                        out[:, lo * P:hi * P], k.psum[bk][:, 0:(hi - lo) * P]), t)
                    done.append(ring.free[s])
            rows = Ring([k.sb(f"{name}_in{j}", BATCH * TROW, ctx=mid) for j in range(3)])
            junk = [k.sb(f"{name}_pick{j}", P, ctx=mid) for j in range(4)]
            jt = [None] * 4
            tail_cols = [st.v(lambda e, t=t: e.memset(t[:, TILES:IT], 0.0)) for t in (sp, dp, sdp)]
            spilled = []
            for j in range(0, TILES, BATCH):
                s, buf, free = rows.take()
                for n in range(BATCH):
                    got = st.dma("gpsimd", lambda e, buf=buf, n=n, j=j: e.indirect_dma_start(
                        buf[:, n * TROW:(n + 1) * TROW], None, table[:, :],
                        bass.IndirectOffsetOnAxis(ap=ed["src"][:, j + n:j + n + 1], axis=0)), k.pool_sems[s], free)
                sc = st.s(lambda e, buf=buf, j=j: e.copy(sp[:, j:j + BATCH].unsqueeze(2), buf[:, :].rearrange(
                    "p (t f) -> p t f", f=TROW)[:, :, TROW - 1:TROW]), got)
                out = st.dma("sync", lambda e, buf=buf, j=j: e.dma_start(spill[:, j * TROW:(j + BATCH) * TROW],
                                                                         buf[:, :]), k.dma_sems[3 + s], got)
                rows.free[s] = [sc, out]
                spilled.append(out)
                hold = []
                st.plain("vector", lambda e, j=j, hold=hold: hold.extend(
                    k.regs(ENG.DVE, ed["blk_row"], j, BATCH, (NB - 1) * P)))
                for n in range(BATCH):
                    for a, (tabl, out_) in enumerate(((dB, dp), (sB, sdp))):
                        z = (2 * n + a) % 4
                        jt[z] = st.v(lambda e, n=n, j=j, z=z, tabl=tabl, out_=out_, hold=hold: e.scalar_tensor_tensor(
                            out=junk[z][:, :], in0=c["node_iota"][:, :], scalar=ed["local"][:, j + n:j + n + 1],
                            in1=tabl[:, bass.ds(hold[n], P)], op0=ALU.is_equal, op1=ALU.mult,
                            accum_out=out_[:, j + n:j + n + 1]), jt[z], done)
            st.wait("sync", spilled[-3:])
            st.run()

        with ExitStack() as soft:
            st = k.stage(name + "_softmax")
            s_scan = k.sb(name + "_s_scan", SLOTS, ctx=soft)
            a = to_scan(k, st, c, s_scan, sp[:, :], [], (2, 3))
            (mx,), done = segment_reduce(k, st, c, ed, soft, name + "_mx", "max", [s_scan], [a])
            mxp = k.sb(name + "_mxp", IT, ctx=soft)
            b_ = to_slots(k, st, c, mxp, lambda g_: mx[:, g_ * P:(g_ + 1) * P], done, (4, 5))
            v = st.v(lambda e: e.tensor_tensor(mxp[:, :], mxp[:, :], sdp[:, :], ALU.max), b_)

            def leaky_sum(dst, a_, b_, tickets):
                q = st.v(lambda e: e.tensor_tensor(dst, a_, b_, ALU.add), tickets)
                return st.v(lambda e: e.scalar_tensor_tensor(out=dst, in0=dst, scalar=0.2, in1=dst, op0=ALU.mult,
                                                             op1=ALU.max), q)
            v = leaky_sum(mxp[:, :], mxp[:, :], dp[:, :], v)
            u = leaky_sum(sp[:, :], sp[:, :], dp[:, :], [a])
            u = st.v(lambda e: e.tensor_tensor(sp[:, :], sp[:, :], mxp[:, :], ALU.subtract), u, v)
            u = st.v(lambda e: e.tensor_scalar(sp[:, :], sp[:, :], 0.0, None, ALU.min), u)
            u = st.s(lambda e: e.activation(sp[:, :], sp[:, :], ACT.Exp), u)
            x_ = leaky_sum(sdp[:, :], sdp[:, :], dp[:, :], v)
            x_ = st.v(lambda e: e.tensor_tensor(sdp[:, :], sdp[:, :], mxp[:, :], ALU.subtract), x_)
            x_ = st.s(lambda e: e.activation(sdp[:, :], sdp[:, :], ACT.Exp), x_)
            a = to_scan(k, st, c, s_scan, sp[:, :], [u, done], (2, 3))
            (tot,), done = segment_reduce(k, st, c, ed, soft, name + "_z", "sum", [s_scan], [a])
            z = to_slots(k, st, c, mxp, lambda g_: tot[:, g_ * P:(g_ + 1) * P], [done, x_], (4, 5))
            z = st.v(lambda e: e.tensor_tensor(mxp[:, :], mxp[:, :], sdp[:, :], ALU.add), z, x_)
            z = st.v(lambda e: e.reciprocal(mxp[:, :], mxp[:, :]), z)
            st.v(lambda e: e.tensor_tensor(sp[:, :], sp[:, :], mxp[:, :], ALU.mult), z, u)
            st.run()

        with ExitStack() as late:
            st = k.stage(name + "_sum")
            rows = Ring([k.sb(f"{name}_back{j}", BATCH * TROW, ctx=late) for j in range(3)])
            hot = Ring([k.sb(f"{name}_hot{j}", P, BF16, ctx=late) for j in range(6)])
            hotw = Ring([k.sb(f"{name}_hotw{j}", P, ctx=late) for j in range(6)])
            bank = Ring([0, 1, 2, 3, 4, 5])
            last_add = st.v(lambda e: e.memset(acc[:, :], 0.0))
            hold, pend = [], []

            def add_up(item):
                nonlocal last_add
                i, bk, slot, product = item
                if i % BATCH == 0:
                    st.plain("vector", lambda e: (hold.clear(), hold.extend(k.regs(ENG.DVE, ed["acc_row"], i, BATCH,
                                                                                   (NB - 1) * ROW))))
                last_add = st.v(lambda e: e.tensor_tensor(acc[:, bass.ds(hold[i % BATCH], ROW)],
                                                          acc[:, bass.ds(hold[i % BATCH], ROW)],
                                                          k.psum[bk][:, 0:ROW], ALU.add), product, own=last_add)
                bank.free[slot] = last_add

            for j in range(0, TILES, BATCH):
                s, buf, free = rows.take()
                got = st.dma("sync", lambda e, buf=buf, j=j: e.dma_start(buf[:, :], spill[:, j * TROW:(j + BATCH) * TROW]),
                             k.dma_sems[s], free)
                for n in range(BATCH):
                    i = j + n
                    hs, ht, hfree = hot.take()
                    made = st.v(lambda e, ht=ht, i=i: e.tensor_scalar(ht[:, :], c["node_iota"][:, :],
                                                                      ed["local"][:, i:i + 1], None, ALU.is_equal), hfree)
                    ws, hw, wfree = hotw.take()
                    scaled = st.s(lambda e, ht=ht, hw=hw, i=i: e.mul(hw[:, :], ht[:, :], sp[:, i:i + 1]), made, wfree)
                    bs, bk, bfree = bank.take()
                    m2 = st.t(lambda e, hw=hw, n=n, buf=buf, bk=bk: e.matmul(
                        k.psum[bk][:, 0:F + 1], hw[:, :], buf[:, n * TROW:n * TROW + F + 1], start=True, stop=True),
                        scaled, got, bfree)
                    hot.free[hs] = scaled
                    hotw.free[ws] = m2
                    pend.append((i, bk, bs, m2))
                    if len(pend) > LAG:
                        add_up(pend.pop(0))
                rows.free[s] = m2
            for item in pend:
                add_up(item)
            st.run()

        st = k.stage(name + "_out")
        acc3 = blocks3(acc, ROW)
        rest = nd(2)
        v = st.v(lambda e: e.tensor_scalar(rest, acc3[:, :, F], -1.0, 1.0, ALU.mult, ALU.add))
        v = st.v(lambda e: e.tensor_scalar(rest, rest, 0.0, None, ALU.max), v)
        v = st.v(lambda e: e.tensor_tensor(blocks3(g), blocks3(g), over(rest, F), ALU.mult), v)
        v = st.v(lambda e: e.tensor_tensor(blocks3(g), blocks3(g), acc3[:, :, 0:F], ALU.add), v)
        v = st.v(lambda e: e.tensor_tensor(blocks3(g), blocks3(g), bias[:, :].unsqueeze(1).to_broadcast([P, NB, F]),
                                           ALU.add), v)
        combine(st, own, g, [v])
        st.run()


def relational_layer(k, c, ed, w, x, acc, tabs):
    left, right, attr_rows, type_rows = tabs
    attr_in = w["attr"]
    with ExitStack() as own:
        idx_l, idx_r = k.sb("idx_l", IT, I32, ctx=own), k.sb("idx_r", IT, I32, ctx=own)
        score = k.sb("score", IT * H, ctx=own)
        edge_w, attp = k.sb("edge_w", 3 * LROW, BF16, ctx=own), k.sb("att_w", HC, BF16, rows=3 * R, ctx=own)
        gate = k.sb("gate", 8 + 4 * R, ctx=own)
        b_row = k.sb("rel_bias", R * F, ctx=own)
        with ExitStack() as pre:
            st = k.stage("rel_tables")
            cols = acc
            wl, bl = k.sb("rel_wl", R * HC, ctx=pre), k.sb("rel_bl", R * HC, ctx=pre)
            att_f, att_parts = score[:, 0:2 * HC], k.sb("att_parts", 3 * HC, BF16, rows=R, ctx=pre)
            att_of_row = score[:, 2 * HC:3 * HC]
            w32, w_rest = score[:, 3 * HC:3 * HC + LROW], score[:, 3 * HC + LROW:3 * HC + 2 * LROW]
            attr32 = score[:, 3 * HC + 2 * LROW:3 * HC + 2 * LROW + EC]
            rel = k.sb("rel_emb", R, rows=DR, ctx=pre)
            wrel = k.sb("rel_we", R * HC, rows=DR, ctx=pre)
            att_all = k.sb("att_all", R * HC, ctx=pre)
            w_lin, b_lin = k.sb("w_lin", R * H, ctx=pre), k.sb("b_lin", R * H, ctx=pre)
            ready = rows_to_cols(k, st, c, x, cols, [])
            tmpi = k.sb("rel_idx", IT, ctx=pre)
            for out, base in ((idx_l, "src"), (idx_r, "dst")):
                v = st.v(lambda e, base=base: e.tensor_copy(tmpi[:, :], ed[base][:, :]), (st.done["vector"], st.done["vector"].count))
                v = st.v(lambda e: e.scalar_tensor_tensor(out=tmpi[:, :], in0=tmpi[:, :], scalar=float(R),
                                                          in1=ed["type"][:, :], op0=ALU.mult, op1=ALU.add), v)
                v = st.v(lambda e, out=out: e.tensor_tensor(out[:, :], tmpi[:, :], ed["valid"][:, :], ALU.mult), v)
            by_feature = w["L2_gnn_W_e"].rearrange("r j f -> j r f")[0:DE]
            for half in range(2):
                st.dma("sync", lambda e, half=half: e.dma_start(w32[half * DE * R:(half + 1) * DE * R, 0:HC], by_feature),
                       k.dma_sems[8])
            for r in range(R):
                st.dma("sync", lambda e, r=r: e.dma_start(wrel[:, r * HC:(r + 1) * HC], w["L2_gnn_W_e"][r, DE:DE + DR, :]), k.dma_sems[8])
                st.dma("sync", lambda e, r=r: e.dma_start(rel[:, r:r + 1], w["L2_gnn_rel_emb"][r].unsqueeze(1)), k.dma_sems[8])
            att_rows = w["L2_gnn_att"].rearrange("r h c -> r (h c)")
            st.dma("sync", lambda e: e.dma_start(att_f[0:R, 0:HC], att_rows), k.dma_sems[8])
            st.dma("sync", lambda e: e.dma_start(att_of_row, att_rows.partition_broadcast(P // R)), k.dma_sems[8])
            st.dma("sync", lambda e: e.dma_start(att_all[:, :], broadcast_row(w["L2_gnn_att"].rearrange("r h c -> (r h c)"))), k.dma_sems[8])
            st.dma("sync", lambda e: e.dma_start(b_row[:, :], broadcast_row(w["L2_gnn_bias"].rearrange("r c -> (r c)"))), k.dma_sems[8])
            gl = st.dma("sync", lambda e: e.dma_start(gate[:, 0:R], broadcast_row(w["L2_gnn_gate"])), k.dma_sems[8])
            a3 = split_bf16(st, att_f[0:R, 0:HC], att_f[0:R, HC:2 * HC],
                            lambda j: att_parts[0:R, j * HC:(j + 1) * HC], [gl])
            for j in range(3):
                packed = st.dma("sync", lambda e, j=j: e.dma_start(attp[j * R:(j + 1) * R, :],
                                                                   att_parts[0:R, j * HC:(j + 1) * HC]), k.dma_sems[9], a3)
            q = st.v(lambda e: e.tensor_tensor(att_of_row, att_of_row, w32[:, 0:HC], ALU.mult), gl)
            q = st.v(lambda e: e.tensor_reduce(w32[:, HC:LROW], att_of_row.rearrange("p (h c) -> p h c", c=F), AX_X,
                                               ALU.add), q)
            q = split_bf16(st, w32, w_rest, lambda j: edge_w[:, j * LROW:(j + 1) * LROW], [q])
            st.v(lambda e: e.tensor_copy(edge_w[0:DE * R, 2 * LROW:3 * LROW], edge_w[0:DE * R, 0:LROW]), q)
            rel_wide = k.sb("rel_wide", R * P, rows=DR, ctx=pre)
            spread = st.v(lambda e: e.tensor_copy(rel_wide[:, :].rearrange("p (r q) -> p r q", q=P), over(rel[:, :], P)), gl)
            gq = lambda a, n=1: gate[:, a:a + n]
            v = st.v(lambda e: e.tensor_reduce(gq(R), gq(0, R), AX_X, ALU.max), gl)
            v = st.v(lambda e: e.tensor_scalar(gq(0, R), gq(0, R), gq(R), None, ALU.subtract), v)
            v = st.s(lambda e: e.activation(gq(8, R), gq(0, R), ACT.Exp), v)
            v = st.v(lambda e: e.tensor_reduce(gq(R + 1), gq(8, R), AX_X, ALU.add), v)
            v = st.v(lambda e: e.reciprocal(gq(R + 2), gq(R + 1)), v)
            v = st.v(lambda e: e.tensor_scalar(gq(8, R), gq(8, R), gq(R + 2), None, ALU.mult), v)
            st.v(lambda e: e.tensor_scalar(gq(8 + R, R), gq(8, R), 1.0 / H, None, ALU.mult), v)
            parts16 = k.sb("attr_parts", 3 * SLOTS, BF16, ctx=pre)

            def split_edges():
                def store(row, j, w, after):
                    return st.dma("scalar", lambda e: e.dma_start(row.rearrange("(p j) -> p j", j=w), part(j, w)),
                                  k.dma_sems[4 + j], after)
                part = lambda j, w=EC: parts16[:, j * SLOTS:j * SLOTS + w]
                t = st.v(lambda e: e.tensor_copy(part(0, SLOTS), ed["type_scan"][:, :]))
                stored_from = [store(type_rows[0], 0, SLOTS, t), None, None]
                for r in range(R):
                    j = 1 + r % 2
                    t = st.v(lambda e, r=r, j=j: e.tensor_scalar(part(j, SLOTS), ed["type_scan"][:, :], float(r), None,
                                                                 ALU.is_equal), stored_from[j])
                    stored_from[j] = store(type_rows[1 + r], j, SLOTS, t)
                v = None
                for f in range(DE):
                    got = st.dma("scalar", lambda e, f=f: e.dma_start(attr32, attr_in[f].rearrange("(p j) -> p j", j=EC)),
                                 k.dma_sems[13], v)
                    v = st.s(lambda e: e.copy(part(0), attr32), got, stored_from)
                    v = st.g(lambda e: e.tensor_tensor(attr32, attr32, part(0), ALU.subtract), v)
                    v = st.s(lambda e: e.copy(part(1), attr32), v)
                    v = st.g(lambda e: e.tensor_tensor(attr32, attr32, part(1), ALU.subtract), v)
                    v = st.s(lambda e: e.copy(part(2), attr32), v)
                    for half, j in enumerate((0, 1, 2, 0)):
                        stored_from[j] = store(attr_rows[half * DE + f], j, EC, v)
                st.wait("scalar", stored_from)
            out_ring = Ring([k.sb(f"rel_out{j}", R * LROW, ctx=pre) for j in range(2)])
            bank = Ring([0, 1, 2, 3, 4])
            bank_lin = Ring([5, 6])
            busy, side_done = v, None
            free_out = lambda: list(out_ring.free)
            for side, (wn, bn, tab) in enumerate((("L2_gnn_W_l", "L2_gnn_b_l", left), ("L2_gnn_W_r", "L2_gnn_b_r", right))):
                for r in range(R):
                    st.dma("scalar", lambda e, r=r, wn=wn: e.dma_start(wl[:, r * HC:(r + 1) * HC], w[wn][r]), k.dma_sems[10],
                           side_done)
                wgot = st.dma("scalar", lambda e, bn=bn: e.dma_start(bl[:, :], broadcast_row(w[bn].rearrange("r f -> (r f)"))),
                              k.dma_sems[10], side_done)
                folded = []
                if side == 1:
                    for r in range(R):
                        m = st.t(lambda e, r=r: e.matmul(k.psum[7][:, 0:HC], rel_wide[:, r * P:(r + 1) * P],
                                                         wrel[:, r * HC:(r + 1) * HC], start=True, stop=True),
                                 spread, gl, folded)
                        folded = [st.v(lambda e, r=r: e.tensor_tensor(bl[:, r * HC:(r + 1) * HC], bl[:, r * HC:(r + 1) * HC],
                                                                      k.psum[7][:, 0:HC], ALU.add), m, wgot)]
                if side == 0:
                    split_edges()
                lin = []
                for src, dst, wide in ((wl, w_lin, P), (bl, b_lin, P)):
                    q = st.v(lambda e, src=src: e.tensor_tensor(out_ring.items[0][:, 0:R * HC], src[:, :],
                                                                att_all[:, :], ALU.mult), wgot, side_done, free_out(), lin, folded)
                    lin = [st.v(lambda e, dst=dst: e.tensor_reduce(
                        dst[:, :], out_ring.items[0][:, 0:R * HC].rearrange("p (h c) -> p h c", c=F), AX_X, ALU.add), q)]
                tview = tab[:, :].rearrange("(b p r) f -> b p (r f)", p=P, r=R)
                for b in range(NB):
                    os_, ob, ofree = out_ring.take()
                    parts = []
                    for r in range(R):
                        bs, bk, bfree = bank.take()
                        m = st.t(lambda e, b=b, r=r, bk=bk: e.matmul(k.psum[bk][:, 0:HC], cols[:, b * P:(b + 1) * P],
                                                                     wl[:, r * HC:(r + 1) * HC], start=True, stop=True),
                                 ready, wgot, bfree, busy)
                        a = st.v(lambda e, r=r, bk=bk, ob=ob: e.tensor_tensor(
                            ob[:, r * LROW:r * LROW + HC], k.psum[bk][:, 0:HC], bl[:, r * HC:(r + 1) * HC], ALU.add),
                            m, wgot, ofree, lin)
                        bank.free[bs] = a
                        parts.append(a)
                    bs, bk, bfree = bank_lin.take()
                    m = st.t(lambda e, b=b, bk=bk: e.matmul(k.psum[bk][:, 0:R * H], cols[:, b * P:(b + 1) * P], w_lin[:, :],
                                                            start=True, stop=True), ready, lin, bfree)
                    a = st.v(lambda e, bk=bk, ob=ob: e.tensor_tensor(
                        ob[:, :].rearrange("p (r f) -> p r f", f=LROW)[:, :, HC:LROW],
                        k.psum[bk][:, 0:R * H].rearrange("p (r h) -> p r h", h=H),
                        b_lin[:, :].rearrange("p (r h) -> p r h", h=H), ALU.add), m, lin, ofree)
                    bank_lin.free[bs] = a
                    parts.append(a)
                    out_ring.free[os_] = st.dma("sync", lambda e, b=b, ob=ob, tview=tview: e.dma_start(tview[b], ob[:, :]),
                                                k.dma_sems[11 + os_], parts)
                side_done = parts
            st.wait("sync", packed, [(k.dma_sems[11 + j], k.dma_sems[11 + j].count) for j in range(2)])
            st.run()

        with ExitStack() as mid:
            st = k.stage("rel_scores")
            NG = 6
            lin = k.sb("lin_score", IT * H, ctx=mid)
            type_of_row = k.sb("type_of_row", 1, ctx=mid)
            tor_i = k.sb("type_of_row_i", 2, I32, ctx=mid)
            sums = Ring([k.sb(f"x_sum{j}", LROW, ctx=mid) for j in range(NG)])
            feats = Ring([k.sb(f"feat{j}", 2 * P, BF16, ctx=mid) for j in range(4)])
            types = Ring([(k.sb(f"types{j}", BATCH * P, BF16, ctx=mid),
                           k.sb(f"type_hot{j}", BATCH * P, BF16, rows=3 * R, ctx=mid)) for j in range(2)])
            masked = Ring([k.sb(f"masked{j}", 2 * P, BF16, ctx=mid) for j in range(3)])
            act_out = Ring([k.sb(f"act_out{j}", HC, ctx=mid) for j in range(3)])
            bank_e, bank_a, bank_l = Ring([0, 1]), Ring([2, 3, 4, 5]), Ring([6, 7])
            a = st.g(lambda e: e.iota(tor_i[:, 0:1], pattern=[[0, 1]], base=0, channel_multiplier=1))
            b1 = st.v(lambda e: e.tensor_scalar(tor_i[:, 1:2], tor_i[:, 0:1], R - 1, None, ALU.bitwise_and), a)
            tor = [st.v(lambda e: e.tensor_copy(type_of_row[:, :], tor_i[:, 1:2]), b1)]
            tor.append(st.v(lambda e: e.memset(score[:, TILES * H:IT * H], 0.0)))
            tor.append(st.v(lambda e: e.memset(lin[:, TILES * H:IT * H], 0.0)))
            hold, waiting = [], []
            ts_ = batch = batch_got = None

            def gather_right(i):
                s, xs, free = sums.take()
                got = st.dma("gpsimd", lambda e: e.indirect_dma_start(
                    xs[:, :], None, right[:, :], bass.IndirectOffsetOnAxis(ap=idx_r[:, i:i + 1], axis=0)), k.pool_sems[s], free)
                return i, s, xs, got

            def add_left(item):
                i, s, xs, got = item
                got = st.dma("gpsimd", lambda e: e.indirect_dma_start(
                    xs[:, :], None, left[:, :], bass.IndirectOffsetOnAxis(ap=idx_l[:, i:i + 1], axis=0),
                    compute_op=ALU.add), k.pool_sems[NG + s], got)
                return i, s, xs, got

            def edge_side(i):
                nonlocal hold, batch, batch_got, ts_
                fs, ft, free = feats.take()
                if i % BATCH == 0:
                    hold = []
                    st.plain("sync", lambda e, hold=hold: hold.extend(k.regs(ENG.SP, ed["edge_row"], i, BATCH, E)))
                    ts_, batch, tfree = types.take()
                    at = slice(i * P, (i + BATCH) * P)
                    st.dma("sync", lambda e, batch=batch: e.dma_start(batch[0][:, :], type_rows[0][at].partition_broadcast(P)),
                           k.dma_sems[12 + ts_], tfree)
                    batch_got = st.dma("sync", lambda e, batch=batch: e.dma_start(batch[1][:, :], type_rows[1:1 + R, at].partition_broadcast(3)),
                                       k.dma_sems[12 + ts_], tfree)
                slots = slice(i % BATCH * P, (i % BATCH + 1) * P)
                ty, hb = batch[0][:, slots], batch[1][:, slots]
                for half in range(2):
                    got = st.dma("sync", lambda e, hold=hold, half=half: e.dma_start(
                        ft[:, half * P:(half + 1) * P], repeat_rows(
                            attr_rows[half * 2 * DE:(half + 1) * 2 * DE, bass.ds(hold[i % BATCH], P)])),
                        k.dma_sems[8 + fs], free)
                ms, mk, mfree = masked.take()
                mm = st.v(lambda e: e.scalar_tensor_tensor(
                    out=mk[:, :].rearrange("p (a q) -> p a q", q=P), in0=ty.unsqueeze(1).to_broadcast([P, 2, P]),
                    scalar=type_of_row[:, 0:1], in1=ft[:, :].rearrange("p (a q) -> p a q", q=P),
                    op0=ALU.is_equal, op1=ALU.mult), got, batch_got, mfree, tor)
                feats.free[fs] = mm
                es, ek, efree = bank_e.take()
                as_, ak, afree = bank_a.take()
                ls, lk, lfree = bank_l.take()
                t2 = st.t(lambda e: e.matmul(k.psum[ak][:, 0:HC], hb, attp[:, :], start=True, stop=True), batch_got, afree)
                for j, half in enumerate((0, 0, 1)):
                    st.t(lambda e, j=j, half=half: e.matmul(
                        k.psum[lk][:, 0:H], mk[:, half * P:(half + 1) * P], edge_w[:, j * LROW + HC:(j + 1) * LROW],
                        start=(j == 0), stop=(j == 2)), mm, lfree)
                    t1 = st.t(lambda e, j=j, half=half: e.matmul(
                        k.psum[ek][:, 0:HC], mk[:, half * P:(half + 1) * P], edge_w[:, j * LROW:j * LROW + HC],
                        start=(j == 0), stop=(j == 2)), efree)
                masked.free[ms] = t1
                types.free[ts_] = [mm, t2]
                return (es, ek, t1), (as_, ak, t2), (ls, lk, t1)

            def activate(item):
                (i, s, xs, got), (es, ek, t1), att, (ls, lk, tl) = item
                l = st.v(lambda e: e.tensor_tensor(lin[:, i * H:(i + 1) * H], xs[:, HC:LROW], k.psum[lk][:, 0:H],
                                                   ALU.add), got, tl, tor)
                bank_l.free[ls] = l
                q = st.v(lambda e: e.tensor_tensor(xs[:, 0:HC], xs[:, 0:HC], k.psum[ek][:, 0:HC], ALU.add), t1)
                bank_e.free[es] = q
                os_, oa, ofree = act_out.take()
                la = st.s(lambda e: e.activation(oa[:, :], xs[:, 0:HC], ACT.Relu, scale=0.8), q, ofree)
                sums.free[s] = [la, l]
                return i, oa, os_, la, att

            def finish(item):
                i, oa, os_, la, (as_, ak, t2) = item
                for h in range(H):
                    d = st.v(lambda e, h=h: e.tensor_tensor_reduce(
                        out=oa[:, h * F:(h + 1) * F], in0=oa[:, h * F:(h + 1) * F],
                        in1=k.psum[ak][:, h * F:(h + 1) * F], scale=1.0, scalar=0.0, op0=ALU.mult, op1=ALU.add,
                        accum_out=score[:, i * H + h:i * H + h + 1]), la, t2)
                act_out.free[os_] = d
                bank_a.free[as_] = d
                return d

            rights, lefts, sides = {}, {}, {}
            for step in range(TILES + 4):
                if step < TILES:
                    rights[step] = gather_right(step)
                if 0 <= step - 2 < TILES:
                    lefts[step - 2] = add_left(rights.pop(step - 2))
                if 0 <= step - 3 < TILES:
                    sides[step - 3] = edge_side(step - 3)
                if 0 <= step - 4 < TILES:
                    waiting.append(activate((lefts.pop(step - 4), *sides.pop(step - 4))))
                    if len(waiting) > 1:
                        finish(waiting.pop(0))
            for item in waiting:
                d = finish(item)
            st.v(lambda e: e.scalar_tensor_tensor(out=score[:, :], in0=lin[:, :], scalar=0.2, in1=score[:, :],
                                                  op0=ALU.mult, op1=ALU.add), d)
            st.run()

        masks = own.enter_context(ExitStack())
        hot = [k.sb(f"is_type{r}", SLOTS, ctx=masks) for r in range(R)]
        pen = [acc[:, r * SLOTS:(r + 1) * SLOTS] for r in range(R)]
        st = k.stage("rel_masks")
        for r in range(R):
            q = st.v(lambda e, r=r: e.tensor_scalar(hot[r][:, :], ed["type_scan"][:, :], float(r), None, ALU.is_equal))
            st.v(lambda e, r=r: e.tensor_scalar(pen[r], hot[r][:, :], -1.0, BIG, ALU.add, ALU.mult), q)
        st.run()
        for h in range(H):
            with ExitStack() as soft:
                st = k.stage(f"rel_soft{h}")
                sc = k.sb("sc_scan", SLOTS, ctx=soft)
                sview = score[:, :].rearrange("q (i h) -> q i h", h=H)[:, :, h]
                a = to_scan(k, st, c, sc, sview, [], (2, 3))
                chans = [acc[:, (R + r) * SLOTS:(R + r + 1) * SLOTS] for r in range(3)]
                chans.append(k.sb("chan3", SLOTS, ctx=soft)[:, :])
                pick = k.sb("picked", SLOTS, ctx=soft)
                half = [st.v, st.g, st.v, st.g]
                t1 = [half[r](lambda e, r=r: e.tensor_tensor(chans[r], pen[r], sc[:, :], ALU.add), a) for r in range(R)]

                def of_own_type(outs, done):
                    v = st.v(lambda e: e.tensor_tensor(pick[:, :], hot[0][:, :], outs[0][:, :], ALU.mult), done[0])
                    for r in range(1, R):
                        u = half[r](lambda e, r=r: e.tensor_tensor(outs[r][:, :], hot[r][:, :], outs[r][:, :], ALU.mult), done[r])
                        v = st.v(lambda e, r=r: e.tensor_tensor(pick[:, :], pick[:, :], outs[r][:, :], ALU.add), u, v)
                    return v
                with ExitStack() as part:
                    outs, done = segment_reduce(k, st, c, ed, part, "rmx", "max", chans, t1)
                    v = of_own_type(outs, done)
                    v = st.v(lambda e: e.tensor_tensor(sc[:, :], sc[:, :], pick[:, :], ALU.subtract), v)
                    v = st.s(lambda e: e.activation(sc[:, :], sc[:, :], ACT.Exp), v)
                    t2 = [half[r](lambda e, r=r: e.tensor_tensor(chans[r], hot[r][:, :], sc[:, :], ALU.mult), v)
                          for r in range(R)]
                    st.run()
                    st = k.stage(f"rel_den{h}")
                    half = [st.v, st.g, st.v, st.g]
                with ExitStack() as part:
                    outs, done = segment_reduce(k, st, c, ed, part, "rsm", "sum", chans, [])
                    v = of_own_type(outs, done)
                    v = st.v(lambda e: e.reciprocal(pick[:, :], pick[:, :]), v)
                    v = st.v(lambda e: e.tensor_tensor(sc[:, :], sc[:, :], pick[:, :], ALU.mult), v)
                    u = st.v(lambda e: e.tensor_scalar(pick[:, :], hot[0][:, :], gate[:, 8 + R:9 + R], None, ALU.mult), v)
                    for r in range(1, R):
                        u = st.v(lambda e, r=r: e.scalar_tensor_tensor(
                            out=pick[:, :], in0=hot[r][:, :], scalar=gate[:, 8 + R + r:9 + R + r], in1=pick[:, :],
                            op0=ALU.mult, op1=ALU.add), u)
                    v = st.v(lambda e: e.tensor_tensor(sc[:, :], sc[:, :], pick[:, :], ALU.mult), u)
                    out = k.sb("w_slots", IT, ctx=part)
                    b_ = to_slots(k, st, c, out, lambda g: sc[:, g * P:(g + 1) * P], [v], (4, 5))
                    st.v(lambda e: e.tensor_copy(sview, out[:, :]), b_)
                    st.run()

        masks.close()
        with ExitStack() as late:
            st = k.stage("rel_sum")
            NG = 6
            rows = Ring([k.sb(f"msg{j}", LROW, ctx=late) for j in range(NG)])
            hot = Ring([k.sb(f"rhot{j}", P, ctx=late) for j in range(5)])
            hotw = Ring([k.sb(f"rhotw{j}", H * P, ctx=late) for j in range(5)])
            bank = Ring([0, 1, 2, 3, 4, 5])
            last_add = st.v(lambda e: e.memset(acc[:, :], 0.0))
            holds, pend = [], []

            def add_up(item):
                nonlocal last_add
                i, bk, slot, product = item
                if i % BATCH == 0:
                    st.plain("vector", lambda e: (holds.clear(), holds.extend(k.regs(ENG.DVE, ed["acc_row"], i, BATCH,
                                                                                     (NB - 1) * ROW))))
                last_add = st.v(lambda e: e.tensor_tensor(acc[:, bass.ds(holds[i % BATCH], F)],
                                                          acc[:, bass.ds(holds[i % BATCH], F)],
                                                          k.psum[bk][:, 0:F], ALU.add), product, own=last_add)
                bank.free[slot] = last_add

            for i in range(TILES):
                s, xl, free = rows.take()
                got = st.dma("gpsimd", lambda e, xl=xl, i=i: e.indirect_dma_start(
                    xl[:, :], None, left[:, :], bass.IndirectOffsetOnAxis(ap=idx_l[:, i:i + 1], axis=0)), k.pool_sems[s], free)
                hs, ht, hfree = hot.take()
                made = st.v(lambda e, ht=ht, i=i: e.tensor_scalar(ht[:, :], c["node_iota"][:, :], ed["local"][:, i:i + 1],
                                                                  None, ALU.is_equal), hfree)
                ws, hw, wfree = hotw.take()
                scaled = []
                for h in range(H):
                    if h < 2:
                        scaled.append(st.v(lambda e, hw=hw, h=h, i=i: e.tensor_scalar(
                            hw[:, h * P:(h + 1) * P], c["node_iota"][:, :], ed["local"][:, i:i + 1],
                            score[:, i * H + h:i * H + h + 1], ALU.is_equal, ALU.mult), wfree))
                    else:
                        scaled.append(st.s(lambda e, ht=ht, hw=hw, h=h, i=i: e.mul(
                            hw[:, h * P:(h + 1) * P], ht[:, :], score[:, i * H + h:i * H + h + 1]), made, wfree))
                bs, bk, bfree = bank.take()
                for h in range(H):
                    m = st.t(lambda e, hw=hw, h=h, xl=xl, bk=bk: e.matmul(
                        k.psum[bk][:, 0:F], hw[:, h * P:(h + 1) * P], xl[:, h * F:(h + 1) * F], start=(h == 0),
                        stop=(h == H - 1)), scaled[h], got, bfree)
                hot.free[hs] = scaled[2:]
                hotw.free[ws] = rows.free[s] = m
                pend.append((i, bk, bs, m))
                if len(pend) > LAG:
                    add_up(pend.pop(0))
            for item in pend:
                add_up(item)
            st.run()

        with ExitStack() as tail:
            st = k.stage("rel_ffn")
            D2 = 2 * F
            par = k.sb("ffn_par", 2, ctx=tail)
            vec = k.sb("ffn_vec", 6 * F, ctx=tail)
            wf1, wf2 = k.sb("ffn_w1", D2, ctx=tail), k.sb("ffn_w2", 2 * F, ctx=tail)
            h1, cols = acc[:, 0:NP], k.sb("ffn_cols", NP, ctx=tail)
            z_ring = Ring([k.sb(f"ffn_z{j}", 8 * P, ctx=tail) for j in range(2)])
            for dst, src in ((wf1[:, :], w["L2_gnn_Wf1"]), (wf2[:, 0:F], w["L2_gnn_Wf2"][0:F, :]),
                             (wf2[:, F:D2], w["L2_gnn_Wf2"][F:D2, :]),
                             (par[:, 0:1], w["L2_gnn_bf1"][0:F].unsqueeze(1)), (par[:, 1:2], w["L2_gnn_bf1"][F:D2].unsqueeze(1)),
                             (vec[:, 0:F], broadcast_row(w["L2_gnn_g1"])), (vec[:, F:2 * F], broadcast_row(w["L2_gnn_bt1"])),
                             (vec[:, 2 * F:3 * F], broadcast_row(w["L2_gnn_g2"])), (vec[:, 3 * F:4 * F], broadcast_row(w["L2_gnn_bt2"])),
                             (vec[:, 4 * F:5 * F], broadcast_row(w["L2_gnn_bf2"]))):
                got = st.dma("sync", lambda e, dst=dst, src=src: e.dma_start(dst, src), k.dma_sems[8])
            brow = vec[:, 5 * F:6 * F]
            v = st.v(lambda e: e.tensor_scalar(brow, b_row[:, 0:F], gate[:, 8:9], None, ALU.mult))
            for r in range(1, R):
                v = st.v(lambda e, r=r: e.scalar_tensor_tensor(out=brow, in0=b_row[:, r * F:(r + 1) * F],
                                                               scalar=gate[:, 8 + r:9 + r], in1=brow, op0=ALU.mult,
                                                               op1=ALU.add), v)
            acc3 = blocks3(acc, ROW)
            v = st.v(lambda e: e.tensor_tensor(blocks3(cols), acc3[:, :, 0:F], brow.unsqueeze(1).to_broadcast([P, NB, F]),
                                               ALU.add), v)
            v = st.v(lambda e: e.tensor_tensor(cols[:, :], cols[:, :], x[:, :], ALU.add), v)
            v = layernorm_rows(k, st, tail, "ln_r1", cols, h1, [v, got], vec[:, 0:F], vec[:, F:2 * F])
            ready = rows_to_cols(k, st, c, h1, cols, [v])
            bank_z, bank_o, done = Ring([0, 1, 2, 3]), Ring([4, 5]), []
            for lo in range(0, NB, 4):
                hi = min(lo + 4, NB)
                wide = (hi - lo) * P
                zslot, z, zfree = z_ring.take()
                zs = []
                for m_ in (0, 1):
                    s, bk, free = bank_z.take()
                    t = st.t(lambda e, lo=lo, bk=bk, m_=m_, wide=wide: e.matmul(
                        k.psum[bk][:, 0:wide], wf1[:, m_ * F:(m_ + 1) * F], cols[:, lo * P:lo * P + wide],
                        start=True, stop=True), ready, free, got)
                    bank_z.free[s] = st.s(lambda e, bk=bk, m_=m_, z=z, wide=wide: e.activation(
                        z[:, m_ * 4 * P:m_ * 4 * P + wide], k.psum[bk][:, 0:wide], ACT.Silu, bias=par[:, m_:m_ + 1]),
                        t, zfree)
                    zs.append(bank_z.free[s])
                s, bk, free = bank_o.take()
                for b in range(lo, hi):
                    for m_ in (0, 1):
                        at = m_ * 4 * P + (b - lo) * P
                        t = st.t(lambda e, b=b, lo=lo, bk=bk, m_=m_, z=z, at=at: e.matmul(
                            k.psum[bk][:, (b - lo) * P:(b - lo + 1) * P], z[:, at:at + P],
                            wf2[:, m_ * F:(m_ + 1) * F], start=(m_ == 0), stop=(m_ == 1)), zs, free)
                z_ring.free[zslot] = t
                q = st.v(lambda e, lo=lo, hi=hi, bk=bk: e.tensor_tensor(
                    cols[:, lo * P:hi * P].rearrange("p (b f) -> p b f", f=F),
                    k.psum[bk][:, 0:(hi - lo) * P].rearrange("p (b f) -> p b f", f=F),
                    vec[:, 4 * F:5 * F].unsqueeze(1).to_broadcast([P, hi - lo, F]), ALU.add), t)
                bank_o.free[s] = q
                done.append(st.v(lambda e, lo=lo, hi=hi: e.tensor_tensor(
                    cols[:, lo * P:hi * P], cols[:, lo * P:hi * P], h1[:, lo * P:hi * P], ALU.add), q))
            v = layernorm_rows(k, st, tail, "ln_r2", cols, h1, done, vec[:, 2 * F:3 * F], vec[:, 3 * F:4 * F])
            v = st.v(lambda e: e.tensor_tensor(h1[:, :], h1[:, :], x[:, :], ALU.add), v)
            layernorm_rows(k, st, tail, "ln2", h1, x, [v])
            st.run()


def gcn_layer(k, c, ed, w, x, acc, table, out):
    with ExitStack() as own:
        h = k.sb("gcn_h", NP, ctx=own)
        dinv = k.sb("gcn_dinv", 2 * NB, ctx=own)
        bias = k.sb("gcn_bias", F, ctx=own)
        with ExitStack() as pre:
            st = k.stage("gcn_nodes")
            cols, wt = k.sb("gcn_cols", NP, ctx=pre), k.sb("gcn_w", F, ctx=pre)
            st.dma("sync", lambda e: e.dma_start(bias[:, :], broadcast_row(w["L3_gnn_b"])), k.dma_sems[8])
            got = st.dma("sync", lambda e: e.dma_start(wt[:, :], w["L3_gnn_W"]), k.dma_sems[8])
            v = st.v(lambda e: e.tensor_scalar(dinv[:, 0:NB], ed["degree"][:, :], 1.0, None, ALU.add))
            v = st.s(lambda e: e.sqrt(dinv[:, NB:2 * NB], dinv[:, 0:NB]), v)
            v = st.v(lambda e: e.reciprocal(dinv[:, 0:NB], dinv[:, NB:2 * NB]), v)
            ready = rows_to_cols(k, st, c, x, cols, [])
            done = linear_rows(k, st, cols, wt[:, :], None, h, [ready, got])
            v = st.v(lambda e: e.tensor_tensor(blocks3(h), blocks3(h), over(dinv[:, 0:NB], F), ALU.mult), v, done)
            o = store_rows(k, st, "sync", table, h, k.dma_sems[9], v)
            st.wait("sync", o)
            st.run()
        aggregate_rows(k, c, ed, "gcn_sum", table, acc, F)
        st = k.stage("gcn_out")
        acc3 = blocks3(acc, ROW)
        v = st.v(lambda e: e.tensor_tensor(blocks3(h), blocks3(h), acc3[:, :, 0:F], ALU.add))
        v = st.v(lambda e: e.tensor_tensor(blocks3(h), blocks3(h), over(dinv[:, 0:NB], F), ALU.mult), v)
        v = st.v(lambda e: e.tensor_tensor(blocks3(h), blocks3(h), bias[:, :].unsqueeze(1).to_broadcast([P, NB, F]),
                                           ALU.add), v)
        v = st.v(lambda e: e.scalar_tensor_tensor(out=h[:, :], in0=h[:, :], scalar=0.0, in1=x[:, :], op0=ALU.max,
                                                  op1=ALU.add), v)
        v = layernorm_rows(k, st, own, "ln3", h, x, [v])
        full = (NB - 1) * P
        st.dma("sync", lambda e: e.dma_start(out[0:full, :].rearrange("(b p) f -> p b f", p=P),
                                             x[:, 0:full].rearrange("p (b f) -> p b f", f=F)), k.dma_sems[10], v)
        o = st.dma("sync", lambda e: e.dma_start(out[full:N, :], x[0:LAST, full:NP]), k.dma_sems[10], v)
        st.wait("sync", o)
        st.run()


def build(nc, w, out, tables):
    with ExitStack() as ctx:
        k = Kernel(nc, ctx)
        c = make_constants(k)
        ed = {"degree": k.sb("degree", NB)}
        x, acc = k.sb("x_rows", NP), k.sb("acc", NB * ROW)
        plan_tiles(k, c, w["dst"], w["recs"], ed)

        st = k.stage("load_x")
        full = (NB - 1) * P
        z = st.v(lambda e: e.memset(x[:, full:NP], 0.0))
        st.dma("sync", lambda e: e.dma_start(x[:, 0:full].rearrange("p (b f) -> p b f", f=F),
                                             w["x"][0:full, :].rearrange("(b p) f -> p b f", p=P)), k.dma_sems[8])
        o = st.dma("sync", lambda e: e.dma_start(x[0:LAST, full:NP], w["x"][full:N, :]), k.dma_sems[8], z)
        st.wait("sync", o)
        st.run()

        gin_layer(k, c, ed, w, x, acc, ed["degree"])

        with ExitStack() as own:
            h = k.sb("gat_h", NP, ctx=own)
            with ExitStack() as pre:
                st = k.stage("gat_in")
                cols, wt = k.sb("gat_in_cols", NP, ctx=pre), k.sb("gat_in_w", F, ctx=pre)
                bn = k.sb("gat_in_b", F, ctx=pre)
                st.dma("sync", lambda e: e.dma_start(bn[:, :], broadcast_row(w["L1_gnn_b_node"])), k.dma_sems[8])
                got = st.dma("sync", lambda e: e.dma_start(wt[:, :], w["L1_gnn_W_node"]), k.dma_sems[8])
                ready = rows_to_cols(k, st, c, x, cols, [])
                linear_rows(k, st, cols, wt[:, :], bn[:, :], h, [ready, got])
                st.run()
            gat_layer(k, c, ed, w, 0, h, acc, tables["gat"], tables["spill"],
                      lambda st, o, g, after: after)

            def residual(st, o, g, after):
                v = st.v(lambda e: e.tensor_tensor(g[:, :], g[:, :], x[:, :], ALU.add), after)
                layernorm_rows(k, st, o, "ln1", g, x, [v])
            gat_layer(k, c, ed, w, 1, h, acc, tables["gat"], tables["spill"], residual)

        relational_layer(k, c, ed, w, x, acc, (tables["left"], tables["right"], tables["attr_rows"],
                                               tables["type_rows"]))
        gcn_layer(k, c, ed, w, x, acc, tables["gcn"], out)


WEIGHTS = ['L0_gnn_eps', 'L0_gnn_W1', 'L0_gnn_b1', 'L0_gnn_gamma1', 'L0_gnn_beta1', 'L0_gnn_a1', 'L0_gnn_W2',
           'L0_gnn_b2', 'L0_gnn_gamma2', 'L0_gnn_beta2', 'L0_gnn_a2', 'L1_gnn_W_node', 'L1_gnn_b_node',
           'L1_gnn_lyr_W', 'L1_gnn_att_src', 'L1_gnn_att_dst', 'L1_gnn_lyr_bias', 'L2_gnn_rel_emb', 'L2_gnn_W_l',
           'L2_gnn_b_l', 'L2_gnn_W_r', 'L2_gnn_b_r', 'L2_gnn_W_e', 'L2_gnn_att', 'L2_gnn_bias', 'L2_gnn_gate',
           'L2_gnn_g1', 'L2_gnn_bt1', 'L2_gnn_g2', 'L2_gnn_bt2', 'L2_gnn_Wf1', 'L2_gnn_bf1', 'L2_gnn_Wf2',
           'L2_gnn_bf2', 'L3_gnn_W', 'L3_gnn_b']


def kernel(**inputs):
    import concourse.bacc as bacc
    from concourse.bass_utils import run_bass_kernel_spmd

    def padded(a, value):
        return np.concatenate([a, np.full((EP - E,), value, a.dtype)])

    src, dst, typ = padded(inputs["src"], 0), padded(inputs["dst"], FAR), padded(inputs["edge_type_4"], 0)
    attr = np.concatenate([inputs["edge_attr_16"].T, np.zeros((DE, EP - E), np.float32)], axis=1)
    arrays = {"x": inputs["x"], "dst": dst, "recs": np.stack([src, dst, typ], axis=1),
              "attr": attr}
    for n in WEIGHTS:
        a = np.asarray(inputs[n])
        arrays[n] = a.reshape(1) if a.ndim == 0 else a
    nc = bacc.Bacc("TRN2", target_bir_lowering=False, num_devices=1)
    w, feed = {}, {}
    for n, a in arrays.items():
        a = np.ascontiguousarray(a)
        feed["in_" + n] = a
        w[n] = nc.dram_tensor("in_" + n, a.shape, mybir.dt.from_np(a.dtype), kind="ExternalInput").ap()
    out = nc.dram_tensor("out", (N, F), F32, kind="ExternalOutput").ap()
    tables = {
        "gat": nc.dram_tensor("gat_table", (NP, TROW), F32, kind="Internal").ap(),
        "gcn": nc.dram_tensor("gcn_table", (NP, F), F32, kind="Internal").ap(),
        "left": nc.dram_tensor("left_table", (NP * R, LROW), F32, kind="Internal").ap(),
        "right": nc.dram_tensor("right_table", (NP * R, LROW), F32, kind="Internal").ap(),
        "attr_rows": nc.dram_tensor("attr_rows", (4 * DE, EP), BF16, kind="Internal").ap(),
        "type_rows": nc.dram_tensor("type_rows", (1 + R, P * SLOTS), BF16, kind="Internal").ap(),
        "spill": nc.dram_tensor("spill", (P, TILES * TROW), F32, kind="Internal").ap(),
    }
    build(nc, w, out, tables)
    return run_bass_kernel_spmd(nc, [feed], core_ids=[0]).results[0]["out"]
```
